# Optimizing a Trainium2 kernel written in Bass

```python
import numpy as np
import jax
import jax.numpy as jnp

def _softmax(x, axis=-1):
    return jax.nn.softmax(x, axis=axis)

def _gelu(x):
    return jax.nn.gelu(x, approximate=True)

def _silu(x):
    return jax.nn.silu(x)

def _sigmoid(x):
    return jax.nn.sigmoid(x)

def _layernorm(x, axis=-1, eps=1e-05):
    m = jnp.mean(x, axis=axis, keepdims=True)
    v = jnp.var(x, axis=axis, keepdims=True)
    return (x - m) / jnp.sqrt(v + eps)

def _scatter_add(tgt, idx, src, axis=0):
    return tgt.at[idx].add(src)

def _segment_sum(src, seg, n):
    return jax.ops.segment_sum(src, seg, n)
kernel_name = 'mk_prb_d1_jaxref_r4_e6b66f'

def setup_inputs(seed: int=0):
    np.random.seed(seed)
    _w = jnp.asarray

    def _L0_attn_setup():
        import jax, jax.numpy as jnp
        import numpy as np
        N_HEAD = 16
        R = 8
        THRESHOLD = 0.1

        def _causal_attention(Q, K, V):
            D = Q.shape[-1]
            scores = jnp.einsum('bhqd,bhkd->bhqk', Q, K) / jnp.sqrt(jnp.asarray(D, Q.dtype))
            T = Q.shape[2]
            causal = jnp.tril(jnp.ones((T, T), dtype=bool))
            scores = jnp.where(causal, scores, jnp.asarray(-jnp.inf, scores.dtype))
            probs = jax.nn.softmax(scores, axis=-1)
            return jnp.einsum('bhqk,bhkd->bhqd', probs, V)
        key = jax.random.key(seed)
        k1, k2, k3 = jax.random.split(key, 3)
        B, T, C = (2, 512, 512)
        fused_dim = 3 * C
        x = jax.random.normal(k1, (B, T, C), dtype=jnp.float32)
        W_attn = jax.random.normal(k2, (fused_dim, C), dtype=jnp.float32) * (1.0 / np.sqrt(C))
        W_proj = jax.random.normal(k3, (C, C), dtype=jnp.float32) * (1.0 / np.sqrt(C))
        w_std = jnp.ones((N_HEAD,), dtype=jnp.float32) * 0.5
        w_rec = jnp.ones((N_HEAD,), dtype=jnp.float32) * 0.3
        return {'x': x, 'W_attn': W_attn, 'W_proj': W_proj, 'w_std': w_std, 'w_rec': w_rec}
    _L0_attn_in = _L0_attn_setup()

    def _L0_ffn_setup():
        import jax, jax.numpy as jnp
        import numpy as np
        B, S, H, I = (1, 64, 512, 1536)

        def _quantized_matmul(x, w, scale):
            wq = w.astype(jnp.float8_e4m3fn).astype(x.dtype)
            y = jnp.einsum('bsi,io->bso', x, wq)
            return y * scale
        key = jax.random.key(seed)
        ks = jax.random.split(key, 7)
        return {'x': jax.random.normal(ks[0], (B, S, H), dtype=jnp.float32), 'gate_w': jax.random.normal(ks[1], (H, I), dtype=jnp.float32) * 0.02, 'up_w': jax.random.normal(ks[2], (H, I), dtype=jnp.float32) * 0.02, 'down_w': jax.random.normal(ks[3], (I, H), dtype=jnp.float32) * 0.02, 'gate_scale': jax.random.uniform(ks[4], (I,), dtype=jnp.float32, minval=0.5, maxval=1.5), 'up_scale': jax.random.uniform(ks[5], (I,), dtype=jnp.float32, minval=0.5, maxval=1.5), 'down_scale': jax.random.uniform(ks[6], (H,), dtype=jnp.float32, minval=0.5, maxval=1.5)}
    _L0_ffn_in = _L0_ffn_setup()
    _d = {'L0_attn_x': _L0_attn_in['x'], 'L0_attn_W_attn': _L0_attn_in['W_attn'], 'L0_attn_W_proj': _L0_attn_in['W_proj'], 'L0_attn_w_std': _L0_attn_in['w_std'], 'L0_attn_w_rec': _L0_attn_in['w_rec'], 'L0_ffn_gate_w': _L0_ffn_in['gate_w'], 'L0_ffn_up_w': _L0_ffn_in['up_w'], 'L0_ffn_down_w': _L0_ffn_in['down_w'], 'L0_ffn_gate_scale': _L0_ffn_in['gate_scale'], 'L0_ffn_up_scale': _L0_ffn_in['up_scale'], 'L0_ffn_down_scale': _L0_ffn_in['down_scale']}
    _x0 = _d['L0_attn_x']
    _d['L0_attn_x'] = jax.random.normal(jax.random.fold_in(jax.random.key(seed), 1), (1, 4096, 512), dtype=_x0.dtype)
    del _x0
    return _d

def reference(L0_attn_x, L0_attn_W_attn, L0_attn_W_proj, L0_attn_w_std, L0_attn_w_rec, L0_ffn_gate_w, L0_ffn_up_w, L0_ffn_down_w, L0_ffn_gate_scale, L0_ffn_up_scale, L0_ffn_down_scale):

    def _L0_attn_ref(x, W_attn, W_proj, w_std, w_rec):
        import jax, jax.numpy as jnp
        import numpy as np
        N_HEAD = 16
        R = 8
        THRESHOLD = 0.1

        def _causal_attention(Q, K, V):
            D = Q.shape[-1]
            scores = jnp.einsum('bhqd,bhkd->bhqk', Q, K) / jnp.sqrt(jnp.asarray(D, Q.dtype))
            T = Q.shape[2]
            causal = jnp.tril(jnp.ones((T, T), dtype=bool))
            scores = jnp.where(causal, scores, jnp.asarray(-jnp.inf, scores.dtype))
            probs = jax.nn.softmax(scores, axis=-1)
            return jnp.einsum('bhqk,bhkd->bhqd', probs, V)
        B, T, C = x.shape
        H = N_HEAD
        head_dim = C // H
        D_std = head_dim - R
        q_std_end = H * D_std
        k_std_end = q_std_end + H * D_std
        v_end = k_std_end + C
        q_low_end = v_end + H * R
        fused = jnp.einsum('btc,fc->btf', x, W_attn)

        def split_heads(a, d):
            return a.reshape(B, T, H, d).transpose(0, 2, 1, 3)
        Q_std = split_heads(fused[..., :q_std_end], D_std)
        K_std = split_heads(fused[..., q_std_end:k_std_end], D_std)
        V = split_heads(fused[..., k_std_end:v_end], head_dim)
        Q_low = split_heads(fused[..., v_end:q_low_end], R)
        K_low = split_heads(fused[..., q_low_end:], R)
        use_ra = (w_rec > THRESHOLD).reshape(1, H, 1, 1)
        ws = jnp.sqrt(jnp.clip(w_std, 1e-08, None)).reshape(1, H, 1, 1)
        wr = jnp.sqrt(jnp.clip(w_rec, 1e-08, None)).reshape(1, H, 1, 1)
        Qf_low = jnp.where(use_ra, wr * K_low, ws * Q_low)
        Kf_low = jnp.where(use_ra, wr * Q_low, ws * K_low)
        Qf = jnp.concatenate([ws * Q_std, Qf_low], axis=-1)
        Kf = jnp.concatenate([ws * K_std, Kf_low], axis=-1)
        out = _causal_attention(Qf, Kf, V)
        out = out.transpose(0, 2, 1, 3).reshape(B, T, C)
        return jnp.einsum('btc,oc->bto', out, W_proj)

    def _L0_ffn_ref(x, gate_w, up_w, down_w, gate_scale, up_scale, down_scale):
        import jax, jax.numpy as jnp
        import numpy as np
        B, S, H, I = (1, 64, 512, 1536)

        def _quantized_matmul(x, w, scale):
            wq = w.astype(jnp.float8_e4m3fn).astype(x.dtype)
            y = jnp.einsum('bsi,io->bso', x, wq)
            return y * scale
        gate = jax.nn.silu(_quantized_matmul(x, gate_w, gate_scale))
        up = _quantized_matmul(x, up_w, up_scale)
        fuse = gate * up
        return _quantized_matmul(fuse, down_w, down_scale)
    x = L0_attn_x
    xn = _layernorm(x, axis=-1)
    x = x + _L0_attn_ref(xn, L0_attn_W_attn, L0_attn_W_proj, L0_attn_w_std, L0_attn_w_rec) + _L0_ffn_ref(xn, L0_ffn_gate_w, L0_ffn_up_w, L0_ffn_down_w, L0_ffn_gate_scale, L0_ffn_up_scale, L0_ffn_down_scale)
    return x

_drawn_inputs = setup_inputs


def setup_inputs(seed=0):
    import zlib

    import numpy as np

    out = dict(_drawn_inputs(seed))
    spreads = {'L0_attn_w_std': (0.5, 0.2), 'L0_attn_w_rec': (0.30000001192092896, 0.6)}
    factors = {}
    for name, (base, spread) in spreads.items():
        noise = np.random.default_rng([zlib.crc32(name.encode()), seed]).standard_normal(out[name].shape)
        drawn = base * np.exp(spread * noise) if base else spread * noise
        out[name] = jnp.asarray(drawn.astype(out[name].dtype))
    for name, factor in factors.items():
        out[name] = (out[name] * factor).astype(out[name].dtype)
    return out
```

```python
import math

import concourse.bass as bass
from concourse import mybir
from contextlib import ExitStack

F32 = mybir.dt.float32
F16 = mybir.dt.float16
BF16 = mybir.dt.bfloat16
F8 = mybir.dt.float8e4
ALU = mybir.AluOpType
ACT = mybir.ActivationFunctionType
AX = mybir.AxisListType

P = 128
T = 4096
C = 512
H = 16
D = C // H
R = 8
DS = D - R
I = 1536
CC = C // P
IT = I // P
QT = 512
NT = T // QT
TB = QT // P
NB = T // P
ROWS = 3 * D
THRESHOLD = 0.1
EPS = 1e-5
MASKED = -1e30
LIFT = 18 * math.log(2.0) * math.sqrt(D)
EXP_SCALE = 1.0 / math.sqrt(D)


def setup_phase(nc, a, keep, ph):
    with ExitStack() as ctx:
        sem = lambda name: ctx.enter_context(nc.semaphore(name))
        sb = lambda name, shape, dt: ctx.enter_context(nc.sbuf_tensor(name, shape, dt))
        stats = sb("stats", [P, NB, 6], F32)
        moments = sb("moments", [P, NB, 2], F32)
        var_eps = sb("var_eps", [P, NB], F32)
        root = sb("root", [P, NB], F32)
        inv_root = sb("inv_root", [P, NB], F32)
        head_w = sb("head_w", [P, 2, H], F32)
        head_c = sb("head_c", [P, 2, H], F32)
        head_r = sb("head_r", [P, 2, H], F32)
        head_i = sb("head_i", [P, 2, H], F32)
        use_ra = sb("use_ra", [P, 2, H], F32)
        low_w = sb("low_w", [P, 2, H], F32)
        low_t = sb("low_t", [P, 2, CC, H, R], F32)
        raw = [ph["fuse_part"][:, k, :, :].rearrange("p i t -> p (i t)").bitcast(F32)[:, 0:CC * C]
               .rearrange("p (c h d) -> p c h d", c=CC, h=H) for k in (0, 1)]
        stage8 = sb("stage8", [P, 2, I], F8)
        stage = [ph["stage"][:, k, :] for k in range(3)]

        x_in = [sem(f"x_in{t}") for t in range(NT)]
        raw_in = sem("raw_in")
        head_in = sem("head_in")
        wv_in = sem("wv_in")
        ffn_in = [sem(f"ffn_in{k}") for k in range(3)]
        ffn_cast = sem("ffn_cast")
        ffn_wide = sem("ffn_wide")
        scales_in = sem("scales_in")
        stats_done = sem("stats_done")
        head_step = sem("head_step")
        var_ready = sem("var_ready")
        root_ready = sem("root_ready")
        hroot_ready = sem("hroot_ready")
        low_done = sem("low_done")
        norm_step = sem("norm_step")
        mask_zero = sem("mask_zero")
        mask_done = sem("mask_done")
        ones_done = sem("ones_done")

        loads = [(a["gate_w"], c, 0) for c in range(CC)] + [(a["up_w"], c, 1) for c in range(CC)] \
            + [(a["down_w"], c, 2) for c in range(CC)]

        def ffn_src(w, c, kind):
            if kind < 2:
                return w[c * P:(c + 1) * P, :]
            return w[c * 3 * P:(c + 1) * 3 * P, :].rearrange("(i p) n -> p i n", p=P)

        def ffn_dst(c, kind):
            if kind < 2:
                return ph["gate_up"][:, kind, c, :]
            return ph["down"][:, 3 * c:3 * c + 3, :].rearrange("p i n -> p (i n)")

        block = ctx.enter_context(nc.Block())

        def cast(act, n):
            _, c, kind = loads[n]
            act.wait_ge(ffn_in[n % 3], 16 * (n // 3 + 1))
            if n >= 2:
                act.wait_ge(ffn_wide, n - 1)
            nc.scalar.activation(stage8[:, n % 2, :], stage[n % 3], ACT.Copy, saturate=False)\
                .then_inc(ffn_cast, 1)

        @block.sync
        def _(sp):
            for t in range(NT):
                sp.dma_start(keep["x"][:, t * TB:(t + 1) * TB, :],
                             a["x"][t * QT:(t + 1) * QT, :].rearrange("(b p) c -> p b c", p=P))\
                    .then_inc(x_in[t], 16)

        @block.gpsimd
        def _(pool):
            nc.gpsimd.memset(keep["ident"][:, :], 0.0).then_inc(mask_zero, 1)
            nc.gpsimd.memset(keep["ident16"][:, :], 0.0).then_inc(mask_zero, 1)
            nc.gpsimd.memset(keep["mask_kq"][:, :], 0.0).then_inc(mask_zero, 1)
            nc.gpsimd.memset(keep["mask_qk"][:, :], 0.0).then_inc(mask_zero, 1)
            nc.gpsimd.memset(ph["v_parts"][:, :, :, 3, :], 1.0).then_inc(ones_done, 1)
            pool.wait_ge(mask_zero, 4)
            for m in (keep["ident"], keep["ident16"]):
                nc.gpsimd.affine_select(out=m[:, :], in_=m[:, :], compare_op=ALU.not_equal, fill=1.0,
                                        base=0, pattern=[[-1, P]], channel_multiplier=1)\
                    .then_inc(mask_done, 1)
            nc.gpsimd.affine_select(out=keep["mask_kq"][:, :], in_=keep["mask_kq"][:, :],
                                    compare_op=ALU.is_ge, fill=MASKED, base=0,
                                    pattern=[[1, P]], channel_multiplier=-1).then_inc(mask_done, 1)
            nc.gpsimd.affine_select(out=keep["mask_qk"][:, :], in_=keep["mask_qk"][:, :],
                                    compare_op=ALU.is_ge, fill=MASKED, base=0,
                                    pattern=[[-1, P]], channel_multiplier=1).then_inc(mask_done, 1)
            for n, (_, c, kind) in enumerate(loads):
                pool.wait_ge(ffn_cast, n + 1)
                nc.gpsimd.tensor_copy(ffn_dst(c, kind), stage8[:, n % 2, :]).then_inc(ffn_wide, 1)

        @block.scalar
        def _(act):
            act.dma_start(head_w[:, 0, :], a["w_std"].partition_broadcast(P)).then_inc(head_in, 16)
            act.dma_start(head_w[:, 1, :], a["w_rec"].partition_broadcast(P)).then_inc(head_in, 16)
            for k in (0, 1):
                act.dma_start(raw[k].rearrange("p c h d -> p c (h d)"),
                              a["w_qk"][k].rearrange("(c p) f -> p c f", p=P)).then_inc(raw_in, 16)
            act.dma_start(ph["w_v"][:, :, :], a["w_v"].rearrange("(c p) f -> p c f", p=P))\
                .then_inc(wv_in, 16)
            act.dma_start(ph["gu_scale"][:, :, :], a["gu_scale"]).then_inc(scales_in, 16)
            act.dma_start(ph["down_scale"][:, :], a["down_scale"].partition_broadcast(P))\
                .then_inc(scales_in, 16)
            for n, (w, c, kind) in enumerate(loads):
                if n >= 3:
                    act.wait_ge(ffn_cast, n - 2)
                act.dma_start(stage[n % 3] if kind < 2 else stage[n % 3].rearrange("p (i n) -> p i n", i=3),
                              ffn_src(w, c, kind)).then_inc(ffn_in[n % 3], 16)
                if n >= 2:
                    cast(act, n - 2)
            cast(act, len(loads) - 2)
            cast(act, len(loads) - 1)
            act.wait_ge(head_step, 1)
            nc.scalar.activation(head_r[:, :, :], head_c[:, :, :], ACT.Sqrt).then_inc(hroot_ready, 1)
            act.wait_ge(var_ready, 1)
            nc.scalar.activation(root[:, :], var_eps[:, :], ACT.Sqrt).then_inc(root_ready, 1)
            act.wait_ge(wv_in, 16)
            act.wait_ge(scales_in, 32)


        @block.vector
        def _(dve):
            dve.wait_ge(head_in, 32)
            nc.vector.tensor_scalar(head_c[:, :, :], head_w[:, :, :], 1e-8, None, ALU.max)\
                .then_inc(head_step, 1)
            nc.vector.tensor_scalar(use_ra[:, 0, :], head_w[:, 1, :], THRESHOLD, None, ALU.is_gt)\
                .then_inc(head_step, 1)
            dve.wait_ge(head_step, 2)
            nc.vector.tensor_scalar(use_ra[:, 1, :], use_ra[:, 0, :], -1.0, 1.0, ALU.mult, ALU.add)\
                .then_inc(head_step, 1)
            for t in range(NT):
                dve.wait_ge(x_in[t], 16)
                for b in range(t * TB, (t + 1) * TB):
                    nc.vector.bn_stats(stats[:, b, :], keep["x"][:, b, :]).then_inc(stats_done, 1)
            dve.wait_ge(stats_done, NB)
            for b in range(NB):
                nc.vector.bn_aggr(moments[:, b, :], stats[:, b, :]).then_inc(stats_done, 1)
            dve.wait_ge(stats_done, 2 * NB)
            nc.vector.tensor_scalar(var_eps[:, :], moments[:, :, 1], EPS, None, ALU.add)\
                .then_inc(var_ready, 1)
            nc.vector.tensor_copy(ph["mean"][:, :], moments[:, :, 0])
            dve.wait_ge(hroot_ready, 1)
            nc.vector.reciprocal(head_i[:, :, :], head_r[:, :, :]).then_inc(head_step, 1)
            dve.wait_ge(head_step, 4)
            nc.vector.tensor_tensor(head_i[:, :, :], head_i[:, :, :], head_c[:, :, :], ALU.mult)\
                .then_inc(head_step, 1)
            dve.wait_ge(head_step, 5)
            nc.vector.tensor_tensor(head_i[:, :, :], head_i[:, :, :], head_r[:, :, :], ALU.add)\
                .then_inc(head_step, 1)
            dve.wait_ge(head_step, 6)
            nc.vector.tensor_scalar(head_r[:, :, :], head_i[:, :, :], 0.5, None, ALU.mult)\
                .then_inc(head_step, 1)
            dve.wait_ge(head_step, 7)
            nc.vector.tensor_tensor(low_w[:, 0, :], head_r[:, 1, :], use_ra[:, 0, :], ALU.mult)\
                .then_inc(head_step, 1)
            nc.vector.tensor_tensor(low_w[:, 1, :], head_r[:, 0, :], use_ra[:, 1, :], ALU.mult)\
                .then_inc(head_step, 1)
            dve.wait_ge(head_step, 9)
            dve.wait_ge(raw_in, 32)

            def spread(row, width):
                return row.unsqueeze(2).broadcast_to([P, H, width])

            for k in (0, 1):
                eff = ph["w_qk"][:, k, :, :].rearrange("p c (h d) -> p c h d", h=H)
                for c in range(CC):
                    nc.vector.tensor_tensor(eff[:, c, :, 0:DS], raw[k][:, c, :, 0:DS],
                                            spread(head_r[:, 0, :], DS), ALU.mult)
                    nc.vector.tensor_tensor(low_t[:, 0, c, :, :], raw[1 - k][:, c, :, DS:D],
                                            spread(low_w[:, 0, :], R), ALU.mult).then_inc(low_done, 1)
                    nc.vector.tensor_tensor(low_t[:, 1, c, :, :], raw[k][:, c, :, DS:D],
                                            spread(low_w[:, 1, :], R), ALU.mult).then_inc(low_done, 1)
                dve.wait_ge(low_done, (3 * k + 2) * CC)
                for c in range(CC):
                    nc.vector.tensor_tensor(eff[:, c, :, DS:D], low_t[:, 0, c, :, :],
                                            low_t[:, 1, c, :, :], ALU.add).then_inc(low_done, 1)
                if k == 0:
                    dve.wait_ge(low_done, 3 * CC)
            dve.wait_ge(root_ready, 1)
            nc.vector.reciprocal(inv_root[:, :], root[:, :]).then_inc(norm_step, 1)
            dve.wait_ge(norm_step, 1)
            nc.vector.tensor_tensor(inv_root[:, :], inv_root[:, :], var_eps[:, :], ALU.mult)\
                .then_inc(norm_step, 1)
            dve.wait_ge(norm_step, 2)
            nc.vector.tensor_tensor(inv_root[:, :], inv_root[:, :], root[:, :], ALU.add)\
                .then_inc(norm_step, 1)
            dve.wait_ge(norm_step, 3)
            nc.vector.tensor_scalar(inv_root[:, :], inv_root[:, :], 0.5, None, ALU.mult)\
                .then_inc(norm_step, 1)
            dve.wait_ge(norm_step, 4)
            nc.vector.reciprocal(ph["rstd"][:, :], inv_root[:, :])


def token_phase(nc, a, keep, ph, scratch):
    with ExitStack() as ctx:
        sem = lambda name: ctx.enter_context(nc.semaphore(name))
        sb = lambda name, shape, dt: ctx.enter_context(nc.sbuf_tensor(name, shape, dt))
        xn = sb("xn", [P, 2, C], F32)
        xt = sb("xt", [P, CC, QT], F32)
        xt_part = sb("xt_part", [P, 2, CC, QT], F16)
        qk_part = sb("qk_part", [P, 2, 2, QT], F16)
        v_rest = sb("v_rest", [P, 2, C], F32)
        gate = xn
        fuse = sb("fuse", [P, 2, QT], F32)
        fuse_rest = sb("fuse_rest", [P, 2, QT], F32)
        ffn_out = v_rest
        ps = [ctx.enter_context(nc.psum_tensor(f"tok_ps{n}", [P, QT], F32)) for n in range(8)]
        turn = ps[0:2]
        acc = ps[2:4]
        gu = [ps[4:6], ps[6:8]]
        w_qk, w_v, v_parts, fuse_part = ph["w_qk"], ph["w_v"], ph["v_parts"], ph["fuse_part"]

        xn_ready = sem("xn_ready")
        turned = sem("turned")
        xt_ready = sem("xt_ready")
        xtl_ready = sem("xtl_ready")
        acc_ready = sem("acc_ready")
        high_ready = sem("high_ready")
        low_ready = sem("low_ready")
        v_mid = sem("v_mid")
        v_low = sem("v_low")
        qk_saved = [sem("qk_saved0"), sem("qk_saved1")]
        v_saved = [sem("v_saved0"), sem("v_saved1")]
        gate_ready = sem("gate_ready")
        up_ready = sem("up_ready")
        silu_ready = sem("silu_ready")
        fuse_ready = sem("fuse_ready")
        fuse_high = sem("fuse_high")
        fuse_rem = sem("fuse_rem")
        fuse_mid = sem("fuse_mid")
        fuse_low = sem("fuse_low")
        down_scaled = sem("down_scaled")
        down_added = sem("down_added")

        NQK = 2 * CC
        NACC = NQK + 2 * TB
        block = ctx.enter_context(nc.Block())

        def low_parts(dve, t, b):
            for c in range(CC):
                n = b * CC + c
                dve.wait_ge(xt_ready, t * CC * TB + (n + 1))
                nc.vector.tensor_tensor(xt_part[:, 1, c, b * P:(b + 1) * P], turn[n % 2][:, 0:P],
                                        xt_part[:, 0, c, b * P:(b + 1) * P], ALU.subtract)\
                    .then_inc(xtl_ready, 1)

        @block.tensor
        def _(pe):
            with pe.Fori(0, NT) as t:
                for b in range(TB):
                    pe.wait_ge(xn_ready, t * TB + (b + 1))
                    for c in range(CC):
                        n = b * CC + c
                        bank = turn[n % 2]
                        if n >= 2:
                            pe.wait_ge(xt_ready, t * CC * TB + (n - 1))
                            pe.wait_ge(xtl_ready, t * CC * TB + (n - 1))
                        nc.tensor.transpose(bank[:, 0:P], xn[:, b % 2, c * P:(c + 1) * P],
                                            keep["ident"][:, :]).then_inc(turned, 1)
                pe.wait_ge(xt_ready, t * CC * TB + CC * TB)
                pe.wait_ge(xtl_ready, t * CC * TB + CC * TB)
                for n in range(NQK + TB):
                    if n >= 2:
                        pe.wait_ge(low_ready, t * (NQK + TB) + (n - 1))
                    else:
                        pe.wait_ge(down_scaled, t * TB + 2 - 1 + n)
                    for c in range(CC):
                        if n < NQK:
                            mm = nc.tensor.matmul(acc[n % 2][:, :],
                                                  w_qk[:, n // CC, c, (n % CC) * P:(n % CC + 1) * P],
                                                  xt[:, c, :], start=(c == 0), stop=(c == CC - 1))
                        else:
                            b = n - NQK
                            mm = nc.tensor.matmul(acc[n % 2][:, :], xt[:, c, b * P:(b + 1) * P],
                                                  w_v[:, c, :], start=(c == 0), stop=(c == CC - 1))
                    mm.then_inc(acc_ready, 1)
                for i in range(IT):
                    for k in (0, 1):
                        if i >= 2:
                            if k == 0:
                                pe.wait_ge(silu_ready, t * IT + (i - 1))
                            else:
                                pe.wait_ge(fuse_ready, t * IT + (i - 1))
                        for c in range(CC):
                            for part in (0, 1):
                                mm = nc.tensor.matmul(gu[k][i % 2][:, :],
                                                      ph["gate_up"][:, k, c, i * P:(i + 1) * P],
                                                      xt_part[:, part, c, :],
                                                      start=(c == 0 and part == 0),
                                                      stop=(c == CC - 1 and part == 1))
                        mm.then_inc(gate_ready if k == 0 else up_ready, 1)
                pe.wait_ge(fuse_mid, t * IT + IT)
                pe.wait_ge(fuse_low, t * IT + IT)
                for b in range(TB):
                    if b >= 2:
                        pe.wait_ge(down_scaled, t * TB + (b + 1))
                    else:
                        pe.wait_ge(low_ready, t * (NQK + TB) + (NQK + TB))
                    for i in range(IT):
                        for part in range(3):
                            mm = nc.tensor.matmul(acc[b % 2][:, :],
                                                  fuse_part[:, part, i, b * P:(b + 1) * P],
                                                  ph["down"][:, i, :],
                                                  start=(i == 0 and part == 0),
                                                  stop=(i == IT - 1 and part == 2))
                    mm.then_inc(acc_ready, 1)

        @block.scalar
        def _(act):
            with act.Fori(0, NT) as t:
                for n in range(CC * TB):
                    b, c = n // CC, n % CC
                    act.wait_ge(turned, t * CC * TB + (n + 1))
                    nc.scalar.activation(xt[:, c, b * P:(b + 1) * P], turn[n % 2][:, 0:P], ACT.Copy)
                    nc.scalar.activation(xt_part[:, 0, c, b * P:(b + 1) * P], turn[n % 2][:, 0:P],
                                         ACT.Copy).then_inc(xt_ready, 1)
                for n in range(NQK):
                    act.wait_ge(acc_ready, t * NACC + (n + 1))
                    act.wait_ge(qk_saved[n % 2], (t * (NQK // 2) + (n // 2 + 1)) * 32)
                    nc.scalar.activation(qk_part[:, n % 2, 0, :], acc[n % 2][:, :], ACT.Copy)\
                        .then_inc(high_ready, 1)
                for b in range(TB):
                    act.wait_ge(acc_ready, t * NACC + (NQK + b + 1))
                    act.wait_ge(v_saved[b % 2], (t * (TB // 2) + (b // 2 + 1)) * 16)
                    nc.scalar.activation(v_parts[:, b % 2, :, 0, :],
                                         acc[b % 2][:, :].rearrange("p (h d) -> p h d", h=H),
                                         ACT.Copy).then_inc(high_ready, 1)
                    act.wait_ge(low_ready, t * (NQK + TB) + (NQK + b + 1))
                    nc.scalar.activation(v_parts[:, b % 2, :, 1, :],
                                         v_rest[:, b % 2, :].rearrange("p (h d) -> p h d", h=H),
                                         ACT.Copy).then_inc(v_mid, 1)
                for i in range(IT + 2):
                    if i < IT:
                        act.wait_ge(gate_ready, t * IT + (i + 1))
                        if i >= 2:
                            act.wait_ge(fuse_ready, t * IT + (i - 1))
                        nc.scalar.activation(gate[:, i % 2, :], gu[0][i % 2][:, :], ACT.Silu,
                                             scale=ph["gu_scale"][:, 0, i:i + 1])\
                            .then_inc(silu_ready, 1)
                    if 1 <= i <= IT:
                        act.wait_ge(fuse_ready, t * IT + i)
                        nc.scalar.activation(fuse_part[:, 0, i - 1, :], fuse[:, (i - 1) % 2, :],
                                             ACT.Copy).then_inc(fuse_high, 1)
                    if i >= 2:
                        act.wait_ge(fuse_rem, t * IT + (i - 1))
                        nc.scalar.activation(fuse_part[:, 1, i - 2, :], fuse_rest[:, i % 2, :],
                                             ACT.Copy).then_inc(fuse_mid, 1)
                act.wait_ge(acc_ready, t * NACC + NACC)

        @block.gpsimd
        def _(pool):
            with pool.Fori(0, NT) as t:
                for i in range(IT + 1):
                    if i < IT:
                        pool.wait_ge(fuse_high, t * IT + (i + 1))
                        if i >= 2:
                            pool.wait_ge(fuse_mid, t * IT + (i - 1))
                            pool.wait_ge(fuse_low, t * IT + (i - 1))
                        nc.gpsimd.tensor_tensor(fuse_rest[:, i % 2, :], fuse[:, i % 2, :],
                                                fuse_part[:, 0, i, :], ALU.subtract)\
                            .then_inc(fuse_rem, 1)
                    if i >= 1:
                        pool.wait_ge(fuse_mid, t * IT + i)
                        nc.gpsimd.tensor_tensor(fuse_part[:, 2, i - 1, :], fuse_rest[:, (i - 1) % 2, :],
                                                fuse_part[:, 1, i - 1, :], ALU.subtract)\
                            .then_inc(fuse_low, 1)

        @block.vector
        def _(dve):
            dve.sem_inc(down_scaled, 2)
            with dve.Fori(0, NT) as t:
                for b in range(TB):
                    if b >= 2:
                        dve.wait_ge(turned, t * CC * TB + CC * (b - 1))
                    nc.vector.tensor_scalar(xn[:, b % 2, :], keep["x"][:, bass.ds(t * TB + b, 1), :]
                                            .rearrange("p b c -> p (b c)"),
                                            ph["mean"][:, bass.ds(t * TB + b, 1)],
                                            ph["rstd"][:, bass.ds(t * TB + b, 1)],
                                            ALU.subtract, ALU.mult).then_inc(xn_ready, 1)
                    if b >= 1:
                        low_parts(dve, t, b - 1)
                low_parts(dve, t, TB - 1)
                for n in range(NQK):
                    dve.wait_ge(high_ready, t * (NQK + TB) + (n + 1))
                    nc.vector.tensor_tensor(qk_part[:, n % 2, 1, :], acc[n % 2][:, :],
                                            qk_part[:, n % 2, 0, :], ALU.subtract)\
                        .then_inc(low_ready, 1)
                for b in range(TB):
                    dve.wait_ge(high_ready, t * (NQK + TB) + (NQK + b + 1))
                    if b >= 2:
                        dve.wait_ge(v_low, t * TB + (b - 1))
                    nc.vector.tensor_tensor(v_rest[:, b % 2, :].rearrange("p (h d) -> p h d", h=H),
                                            acc[b % 2][:, :].rearrange("p (h d) -> p h d", h=H),
                                            v_parts[:, b % 2, :, 0, :], ALU.subtract)\
                        .then_inc(low_ready, 1)
                    dve.wait_ge(v_mid, t * TB + (b + 1))
                    nc.vector.tensor_tensor(v_parts[:, b % 2, :, 2, :],
                                            v_rest[:, b % 2, :].rearrange("p (h d) -> p h d", h=H),
                                            v_parts[:, b % 2, :, 1, :], ALU.subtract)\
                        .then_inc(v_low, 1)
                for i in range(IT):
                    dve.wait_ge(up_ready, t * IT + (i + 1))
                    dve.wait_ge(silu_ready, t * IT + (i + 1))
                    if i >= 2:
                        dve.wait_ge(fuse_rem, t * IT + (i - 1))
                    nc.vector.scalar_tensor_tensor(out=fuse[:, i % 2, :], in0=gu[1][i % 2][:, :],
                                                   scalar=ph["gu_scale"][:, 1, i:i + 1],
                                                   in1=gate[:, i % 2, :], op0=ALU.mult, op1=ALU.mult)\
                        .then_inc(fuse_ready, 1)
                for b in range(TB):
                    dve.wait_ge(acc_ready, t * NACC + (NQK + TB + b + 1))
                    if b >= 2:
                        dve.wait_ge(down_added, t * TB + (b - 1))
                    nc.vector.tensor_tensor(ffn_out[:, b % 2, :], acc[b % 2][:, :],
                                            ph["down_scale"][:, :], ALU.mult).then_inc(down_scaled, 1)
                    dve.wait_ge(down_scaled, t * TB + (b + 1 + 2))
                    xb = keep["x"][:, bass.ds(t * TB + b, 1), :].rearrange("p b c -> p (b c)")
                    nc.vector.tensor_tensor(xb, xb, ffn_out[:, b % 2, :], ALU.add)\
                        .then_inc(down_added, 1)


        @block.sync
        def _(sp):
            for k in (0, 1):
                sp.sem_inc(qk_saved[k], 32)
                sp.sem_inc(v_saved[k], 16)
            with sp.Fori(0, NT) as t:
                for n in range(NQK):
                    sp.wait_ge(low_ready, t * (NQK + TB) + (n + 1))
                    for part in (0, 1):
                        sp.dma_start(scratch["qk"][n // CC, part, (n % CC) * P:(n % CC + 1) * P,
                                                   bass.ds(t * QT, QT)],
                                     qk_part[:, n % 2, part, :]).then_inc(qk_saved[n % 2], 16)
                for b in range(TB):
                    sp.wait_ge(v_low, t * TB + (b + 1))
                    sp.dma_start(scratch["v"][bass.ds(t * QT + b * P, P), :, :],
                                 v_parts[:, b % 2, :, :, :].rearrange("p h k d -> p h (k d)"))\
                        .then_inc(v_saved[b % 2], 16)
            for k in (0, 1):
                sp.wait_ge(qk_saved[k], (NT * (NQK // 2) + 1) * 32)
                sp.wait_ge(v_saved[k], (NT * (TB // 2) + 1) * 16)


def score_pairs():
    pairs = []
    for i in range(NT):
        for j in range(0, TB * i, 2):
            pairs.append((i, [(j, 0, 0, QT, False), (j + 1, 0, QT, QT, False)]))
        j = TB * i
        pairs.append((i, [(j, 0, 0, QT, True), (j + 1, P, QT, QT - P, True)]))
        pairs.append((i, [(j + 2, 2 * P, 0, QT - 2 * P, True), (j + 3, 3 * P, 2 * P, QT - 3 * P, True)]))
    return pairs


def max_chunks():
    chunks = []
    for r in range(NB):
        for k in range(0, (r + 1) * P, QT):
            width = min(QT, (r + 1) * P - k)
            chunks.append((r, k, width, k + width == (r + 1) * P))
    return chunks


PAIRS = score_pairs()
CHUNKS = max_chunks()
NPAIR = len(PAIRS)
NCHUNK = len(CHUNKS)
FIRST_SLOT = 4
LAST_SLOT = NPAIR - 4
PV_LAG = 2
OUT_LAG = 1
NP_BUF = 4
SPLIT = QT


def chunks_at(slot):
    span = LAST_SLOT - FIRST_SLOT
    lo, hi = (min(max((s - FIRST_SLOT) * NCHUNK // span, 0), NCHUNK) for s in (slot, slot + 1))
    return range(lo, hi)


def attention_phase(nc, keep, scratch):
    with ExitStack() as ctx:
        sem = lambda name: ctx.enter_context(nc.semaphore(name))
        sb = lambda name, shape, dt: ctx.enter_context(nc.sbuf_tensor(name, shape, dt))
        q_sb = [sb(f"q_sb{k}", [P, T], F16) for k in (0, 1)]
        k_sb = [sb(f"k_sb{k}", [P, T], F16) for k in (0, 1)]
        v_sb = [sb(f"v_sb{k}", [P, NB, P], BF16) for k in (0, 1)]
        probs = sb("probs", [P, NP_BUF, 2 * QT], F32)
        probs_low = sb("probs_low", [P, NP_BUF, 2 * QT], F16)
        out_sb = sb("out_sb", [P, 2, QT], F32)
        row_max = sb("row_max", [P, NB, NT], F32)
        head_max = sb("head_max", [P, NB], F32)
        shift = sb("shift", [NB, P], F16)
        scores = [ctx.enter_context(nc.psum_tensor(f"scores{n}", [P, 2 * QT], F32)) for n in (0, 1)]
        search = [ctx.enter_context(nc.psum_tensor(f"search{n}", [P, QT], F32)) for n in (0, 1)]
        out_ps = [ctx.enter_context(nc.psum_tensor(f"out_ps{n}", [P, QT], F32)) for n in (0, 1)]
        probs_high = probs[:, :, :].rearrange("p b q -> p (b q)").bitcast(BF16)\
            .rearrange("p (b q two) -> p b q two", b=NP_BUF, two=2)

        filled = sem("filled")
        qk_loaded = [sem("qk_loaded0"), sem("qk_loaded1")]
        v_loaded = [sem("v_loaded0"), sem("v_loaded1")]
        shift_loaded = [sem("shift_loaded0"), sem("shift_loaded1")]
        scores_ready = sem("scores_ready")
        exp_done = sem("exp_done")
        low_pool = sem("low_pool")
        low_dve = sem("low_dve")
        pv_done = sem("pv_done")
        out_copied = sem("out_copied")
        out_saved = [sem("out_saved0"), sem("out_saved1")]
        search_ready = sem("search_ready")
        search_used = sem("search_used")
        max_ready = sem("max_ready")
        max_turned = sem("max_turned")
        shift_ready = sem("shift_ready")

        block = ctx.enter_context(nc.Block())

        def pe_search(pe, base, b, c):
            r, k, width, diag = CHUNKS[c]
            bank = search[c % 2]
            if c == 0:
                pe.wait_ge(qk_loaded[b], base["loads"][b])
                if base is not first:
                    pe.wait_ge(shift_ready, base["head"])
            if c >= 2:
                pe.wait_ge(search_used, base["chunk"] + (c - 1))
            mm = nc.tensor.matmul(bank[:, 0:width], q_sb[b][0:ROWS, r * P:(r + 1) * P],
                                  k_sb[b][0:ROWS, k:k + width], start=True, stop=not diag)
            if diag:
                mm = nc.tensor.matmul(bank[:, width - P:width], keep["ident16"][:, :],
                                      keep["mask_qk"][:, :], start=False, stop=True)
            mm.then_inc(search_ready, 1)

        def dve_search(dve, base, c):
            r, k, width, _ = CHUNKS[c]
            dve.wait_ge(search_ready, base["chunk"] + (c + 1))
            nc.vector.reduce_max(row_max[:, r, k // QT:k // QT + 1], search[c % 2][:, 0:width], AX.X)\
                .then_inc(search_used, 1)

        def dve_max(dve, base):
            dve.wait_ge(search_used, base["chunk"] + NCHUNK)
            nc.vector.reduce_max(head_max[:, :], row_max[:, :, :], AX.X).then_inc(max_ready, 1)

        def pe_turn(pe, base):
            pe.wait_ge(max_ready, base["head"] + 1)
            nc.tensor.transpose(search[0][0:NB, 0:P], head_max[:, :], keep["ident"][:, :])\
                .then_inc(max_turned, 1)

        def dve_shift(dve, base, b):
            dve.wait_ge(max_turned, base["head"] + 1)
            dve.wait_ge(shift_loaded[1 - b], base["shifts"][1 - b])
            nc.vector.tensor_scalar(shift[:, :], search[0][0:NB, 0:P], -1.0, LIFT, ALU.mult, ALU.add)\
                .then_inc(shift_ready, 1)

        def sp_shift(sp, base, b):
            sp.wait_ge(shift_ready, base["head"] + 1)
            sp.dma_start(q_sb[b][ROWS:ROWS + 1, :],
                         shift[:, :]).then_inc(shift_loaded[b], 16)

        def sp_load(sp, head, b):
            rows = bass.ds(head * D, D)
            for at, part in ((0, 0), (1, 0), (2, 1)):
                sp.dma_start(q_sb[b][at * D:(at + 1) * D, :], scratch["qk"][0, part, rows, :])\
                    .then_inc(qk_loaded[b], 16)
            for at, part in ((0, 0), (1, 1), (2, 0)):
                sp.dma_start(k_sb[b][at * D:(at + 1) * D, :], scratch["qk"][1, part, rows, :])\
                    .then_inc(qk_loaded[b], 16)
            sp.dma_start(v_sb[b][:, :, :], scratch["v"].rearrange("(n p) h m -> p n h m", p=P)
                         [:, :, bass.ds(head, 1), :].rearrange("p n h m -> p n (h m)"))\
                .then_inc(v_loaded[b], 16)

        def search_base(it, s):
            b = 1 - s
            return {"chunk": it * (2 * NCHUNK) + (s + 1) * NCHUNK, "head": it * 2 + (s + 1),
                    "loads": {b: (it + (1 if s == 0 else 2)) * 96},
                    "shifts": {s: (it + 1) * 16}}

        first = {"chunk": 0, "head": 0, "loads": {0: 96}, "shifts": {1: 0}}

        @block.gpsimd
        def _(pool):
            for b in (0, 1):
                nc.gpsimd.memset(k_sb[b][ROWS:ROWS + 1, :], 1.0).then_inc(filled, 1)
                pool.wait_ge(filled, b + 1)
            nc.gpsimd.memset(row_max[:, :, :], MASKED).then_inc(filled, 1)
            with pool.Fori(0, H // 2) as it:
                for s in (0, 1):
                    for k in range(NPAIR):
                        n = s * NPAIR + k
                        pool.wait_ge(exp_done, it * (2 * NPAIR) + (n + 1))
                        pool.wait_ge(pv_done, it * (2 * NPAIR) + (n + 1))
                        width = min(SPLIT, sum(st[3] for st in PAIRS[k][1]))
                        nc.gpsimd.tensor_tensor(probs_low[:, n % NP_BUF, 0:width],
                                                probs[:, n % NP_BUF, 0:width],
                                                probs_high[:, n % NP_BUF, 0:width, 1],
                                                ALU.subtract).then_inc(low_pool, 1)

        @block.tensor
        def _(pe):
            pe.sem_inc(pv_done, NP_BUF)
            pe.wait_ge(filled, 3)
            for c in range(NCHUNK):
                pe_search(pe, first, 0, c)
            pe_turn(pe, first)
            with pe.Fori(0, H // 2) as it:
                def score_pair(n):
                    s, k = divmod(n, NPAIR)
                    if k == 0:
                        pe.wait_ge(shift_loaded[s], (it + 1) * 16)
                    if n >= 2:
                        pe.wait_ge(exp_done, it * (2 * NPAIR) + (n - 1))
                    i, steps = PAIRS[k]
                    for j, q0, col, width, diag in steps:
                        out = scores[n % 2][:, col:col + width]
                        mm = nc.tensor.matmul(out, k_sb[s][0:ROWS + 1, j * P:(j + 1) * P],
                                              q_sb[s][0:ROWS + 1, i * QT + q0:(i + 1) * QT],
                                              start=True, stop=not diag)
                        if diag:
                            mm = nc.tensor.matmul(out[:, 0:P], keep["ident16"][:, :],
                                                  keep["mask_kq"][:, :], start=False, stop=True)
                    mm.then_inc(scores_ready, 1)

                def product_pair(n):
                    s, k = divmod(n, NPAIR)
                    i, steps = PAIRS[k]
                    tile = s * NT + i
                    if k == 0:
                        pe.wait_ge(v_loaded[s], (it + 1) * 16)
                    if steps[0][0] == 0:
                        pe.wait_ge(out_copied, it * (2 * NT) + (tile + 1))
                    pe.wait_ge(low_pool, it * (2 * NPAIR) + (n + 1))
                    if sum(st[3] for st in steps) > SPLIT:
                        pe.wait_ge(low_dve, it * (2 * NDVE) + (dve_before(n) + 1))
                    for j, q0, col, width, _ in steps:
                        for part in (0, 1):
                            rhs = (probs_high[:, n % NP_BUF, col:col + width, 1] if part == 0
                                   else probs_low[:, n % NP_BUF, col:col + width])
                            mm = nc.tensor.matmul(out_ps[tile % 2][:, q0:QT], v_sb[s][:, j, :], rhs,
                                                  start=(j == 0 and part == 0),
                                                  stop=(j == TB * (i + 1) - 1 and part == 1))
                    mm.then_inc(pv_done, 1)

                score_pair(0)
                for n in range(2 * NPAIR + PV_LAG):
                    if n + 1 < 2 * NPAIR:
                        score_pair(n + 1)
                    if n < 2 * NPAIR:
                        s, k = divmod(n, NPAIR)
                        base = search_base(it, s)
                        for c in chunks_at(k):
                            pe_search(pe, base, 1 - s, c)
                        if k == LAST_SLOT:
                            pe_turn(pe, base)
                    if n >= PV_LAG:
                        product_pair(n - PV_LAG)

        @block.vector
        def _(dve):
            dve.wait_ge(filled, 3)
            for c in range(NCHUNK):
                dve_search(dve, first, c)
            dve_max(dve, first)
            dve.wait_ge(max_turned, 1)
            nc.vector.tensor_scalar(shift[:, :], search[0][0:NB, 0:P], -1.0, LIFT, ALU.mult, ALU.add)\
                .then_inc(shift_ready, 1)
            with dve.Fori(0, H // 2) as it:
                for n in range(2 * NPAIR):
                    s, k = divmod(n, NPAIR)
                    base = search_base(it, s)
                    for c in chunks_at(k):
                        dve_search(dve, base, c)
                    if k == LAST_SLOT - 1:
                        dve_max(dve, base)
                    if k == LAST_SLOT + 1:
                        dve_shift(dve, base, 1 - s)
                    total = sum(st[3] for st in PAIRS[k][1])
                    if total > SPLIT:
                        dve.wait_ge(exp_done, it * (2 * NPAIR) + (n + 1))
                        dve.wait_ge(pv_done, it * (2 * NPAIR) + (n + 1))
                        nc.vector.tensor_tensor(probs_low[:, n % NP_BUF, SPLIT:total],
                                                probs[:, n % NP_BUF, SPLIT:total],
                                                probs_high[:, n % NP_BUF, SPLIT:total, 1],
                                                ALU.subtract).then_inc(low_dve, 1)

        @block.scalar
        def _(act):
            act.sem_inc(out_copied, 2)
            with act.Fori(0, H // 2) as it:
                for n in range(2 * NPAIR + PV_LAG + OUT_LAG):
                    if n < 2 * NPAIR:
                        s, k = divmod(n, NPAIR)
                        width = sum(st[3] for st in PAIRS[k][1])
                        act.wait_ge(scores_ready, it * (2 * NPAIR) + (n + 1))
                        act.wait_ge(pv_done, it * (2 * NPAIR) + (n + 1))
                        nc.scalar.activation(probs[:, n % NP_BUF, 0:width], scores[n % 2][:, 0:width],
                                             ACT.Exp, scale=EXP_SCALE).then_inc(exp_done, 1)
                    m = n - PV_LAG - OUT_LAG
                    if m >= 0 and (m % NPAIR == NPAIR - 1 or PAIRS[m % NPAIR][0] != PAIRS[m % NPAIR + 1][0]):
                        tile = (m // NPAIR) * NT + PAIRS[m % NPAIR][0]
                        act.wait_ge(pv_done, it * (2 * NPAIR) + (m + 1 + NP_BUF))
                        act.wait_ge(out_saved[tile % 2], it * (NT * 16) + (tile // 2 + 1) * 16)
                        nc.scalar.activation(out_sb[:, tile % 2, :], out_ps[tile % 2][:, :], ACT.Copy)\
                            .then_inc(out_copied, 1)

        @block.sync
        def _(sp):
            for b in (0, 1):
                sp.sem_inc(out_saved[b], 16)
            sp_load(sp, 0, 0)
            sp_shift(sp, first, 0)
            with sp.Fori(0, H // 2) as it:
                for s in (0, 1):
                    sp.wait_ge(pv_done, it * (2 * NPAIR) + (s * NPAIR + NP_BUF))
                    sp_load(sp, it * 2 + 1 if s == 0 else (it * 2 + 2) % H, 1 - s)
                    for i in range(NT):
                        tile = s * NT + i
                        if i == NT - 1:
                            sp_shift(sp, search_base(it, s), 1 - s)
                        sp.wait_ge(out_copied, it * (2 * NT) + (tile + 1 + 2))
                        sp.dma_start(scratch["out"][:, bass.ds(it * (2 * D) + s * D, D), i * QT:(i + 1) * QT],
                                     out_sb[:, tile % 2, :]).then_inc(out_saved[tile % 2], 16)
            for b in (0, 1):
                sp.wait_ge(out_saved[b], ((H // 2) * NT + 1) * 16)
                sp.wait_ge(v_loaded[b], (H // 2 + 1 - b) * 16)
                sp.wait_ge(shift_loaded[b], (H // 2 + 1 - b) * 16)


def dve_before(n):
    return sum(1 for m in range(n) if sum(st[3] for st in PAIRS[m % NPAIR][1]) > SPLIT)


NDVE = dve_before(NPAIR)


def output_phase(nc, a, keep, scratch, out):
    with ExitStack() as ctx:
        sem = lambda name: ctx.enter_context(nc.semaphore(name))
        sb = lambda name, shape, dt: ctx.enter_context(nc.sbuf_tensor(name, shape, dt))
        w_proj = sb("w_proj", [P, CC, C], F32)
        parts = sb("parts", [P, 2, CC, 4, QT], F32)
        attn = sb("attn", [P, 2, CC, QT], F32)
        ps = [ctx.enter_context(nc.psum_tensor(f"proj_ps{n}", [P, C], F32)) for n in range(4)]
        w_in = sem("w_in")
        parts_in = [sem("parts_in0"), sem("parts_in1")]
        summed = sem("summed")
        attn_step = sem("attn_step")
        proj_ready = sem("proj_ready")
        y_ready = sem("y_ready")
        y_saved = sem("y_saved")
        block = ctx.enter_context(nc.Block())

        def add_tile(dve, t):
            for b in range(t * TB, (t + 1) * TB):
                dve.wait_ge(proj_ready, b + 1)
                nc.vector.tensor_tensor(keep["x"][:, b, :], ps[b % 4][:, :], keep["x"][:, b, :], ALU.add)\
                    .then_inc(y_ready, 1)

        @block.sync
        def _(sp):
            for t in range(NT):
                if t >= 2:
                    sp.wait_ge(attn_step, 3 * (t - 1))
                for c in range(CC):
                    sp.dma_start(parts[:, t % 2, c, :, :],
                                 scratch["out"][:, c * P:(c + 1) * P, t * QT:(t + 1) * QT]
                                 .rearrange("k r q -> r k q")).then_inc(parts_in[t % 2], 16)

        @block.gpsimd
        def _(pool):
            for t in range(NT):
                pool.wait_ge(parts_in[t % 2], 16 * CC * (t // 2 + 1))
                nc.gpsimd.tensor_tensor(parts[:, t % 2, :, 0, :], parts[:, t % 2, :, 0, :],
                                        parts[:, t % 2, :, 1, :], ALU.add).then_inc(summed, 1)

        @block.vector
        def _(dve):
            for t in range(NT):
                dve.wait_ge(parts_in[t % 2], 16 * CC * (t // 2 + 1))
                pt = parts[:, t % 2, :, :, :]
                nc.vector.reciprocal(pt[:, :, 3, :], pt[:, :, 3, :]).then_inc(attn_step, 1)
                dve.wait_ge(summed, t + 1)
                nc.vector.tensor_tensor(pt[:, :, 0, :], pt[:, :, 0, :], pt[:, :, 2, :], ALU.add)\
                    .then_inc(attn_step, 1)
                dve.wait_ge(attn_step, 3 * t + 2)
                if t >= 2:
                    dve.wait_ge(proj_ready, TB * (t - 1))
                nc.vector.tensor_tensor(attn[:, t % 2, :, :], pt[:, :, 0, :], pt[:, :, 3, :], ALU.mult)\
                    .then_inc(attn_step, 1)
                if t >= 1:
                    add_tile(dve, t - 1)
            add_tile(dve, NT - 1)


        @block.tensor
        def _(pe):
            pe.wait_ge(w_in, 16)
            for t in range(NT):
                pe.wait_ge(attn_step, 3 * (t + 1))
                for b in range(t * TB, (t + 1) * TB):
                    if b >= 4:
                        pe.wait_ge(y_ready, b - 3)
                    for c in range(CC):
                        mm = nc.tensor.matmul(ps[b % 4][:, :],
                                              attn[:, t % 2, c, (b % TB) * P:(b % TB + 1) * P],
                                              w_proj[:, c, :], start=(c == 0), stop=(c == CC - 1))
                    mm.then_inc(proj_ready, 1)

        @block.scalar
        def _(act):
            act.dma_start(w_proj[:, :, :], a["w_proj"].rearrange("(c p) f -> p c f", p=P)).then_inc(w_in, 16)
            for t in range(NT):
                act.wait_ge(y_ready, (t + 1) * TB)
                act.dma_start(out[t * QT:(t + 1) * QT, :].rearrange("(b p) c -> p b c", p=P),
                              keep["x"][:, t * TB:(t + 1) * TB, :]).then_inc(y_saved, 16)
            act.wait_ge(y_saved, 16 * NT)


def build(nc, a, out):
    scratch = {
        "qk": nc.dram_tensor("qk_scratch", (2, 2, C, T), F16).ap(),
        "v": nc.dram_tensor("v_scratch", (T, H, P), BF16).ap(),
        "out": nc.dram_tensor("out_scratch", (4, C, T), F32).ap(),
    }
    with ExitStack() as ctx:
        sb = lambda c, name, shape, dt: c.enter_context(nc.sbuf_tensor(name, shape, dt))
        keep = {
            "x": sb(ctx, "x_sb", [P, NB, C], F32),
            "ident": sb(ctx, "ident", [P, P], F32),
            "ident16": sb(ctx, "ident16", [P, P], BF16),
            "mask_kq": sb(ctx, "mask_kq", [P, P], BF16),
            "mask_qk": sb(ctx, "mask_qk", [P, P], BF16),
        }
        with ExitStack() as early:
            ph = {
                "w_qk": sb(early, "w_qk_sb", [P, 2, CC, C], F32),
                "w_v": sb(early, "w_v_sb", [P, CC, C], F32),
                "gate_up": sb(early, "gate_up", [P, 2, CC, I], BF16),
                "down": sb(early, "down", [P, IT, C], BF16),
                "gu_scale": sb(early, "gu_scale_sb", [P, 2, IT], F32),
                "down_scale": sb(early, "down_scale_sb", [P, C], F32),
                "mean": sb(early, "mean", [P, NB], F32),
                "rstd": sb(early, "rstd", [P, NB], F32),
                "v_parts": sb(early, "v_parts", [P, 2, H, 4, D], BF16),
                "fuse_part": sb(early, "fuse_part", [P, 3, IT, QT], BF16),
            }
            with ExitStack() as st:
                ph["stage"] = sb(st, "stage", [P, 3, I], F32)
                setup_phase(nc, a, keep, ph)
            token_phase(nc, a, keep, ph, scratch)
        attention_phase(nc, keep, scratch)
        output_phase(nc, a, keep, scratch, out)


def kernel(**inputs):
    import numpy as _np
    import concourse.bacc as _bacc
    from concourse import mybir as _mybir
    from concourse.bass_utils import run_bass_kernel_spmd as _run

    arr = {n: _np.asarray(v) for n, v in inputs.items()}
    w = arr["L0_attn_W_attn"]
    q_std, k_std, v, q_low, k_low = _np.split(w, [H * DS, 2 * H * DS, 2 * H * DS + C, 2 * H * DS + C + H * R])
    by_head = lambda std, low: _np.concatenate(
        [std.reshape(H, DS, C), low.reshape(H, R, C)], axis=1).reshape(C, C).T
    data = {
        "x": arr["L0_attn_x"].reshape(T, C),
        "w_qk": _np.stack([by_head(q_std, q_low), by_head(k_std, k_low)]),
        "w_v": v.T,
        "w_proj": arr["L0_attn_W_proj"].T,
        "w_std": arr["L0_attn_w_std"],
        "w_rec": arr["L0_attn_w_rec"],
        "gate_w": arr["L0_ffn_gate_w"],
        "up_w": arr["L0_ffn_up_w"],
        "down_w": arr["L0_ffn_down_w"],
        "gu_scale": _np.stack([arr["L0_ffn_gate_scale"].reshape(IT, P).T,
                               arr["L0_ffn_up_scale"].reshape(IT, P).T], axis=1),
        "down_scale": arr["L0_ffn_down_scale"],
    }
    data = {n: _np.ascontiguousarray(v) for n, v in data.items()}
    nc = _bacc.Bacc("TRN2", target_bir_lowering=False, num_devices=1)
    args = {n: nc.dram_tensor(f"in_{n}", v.shape, _mybir.dt.from_np(v.dtype), kind="ExternalInput").ap()
            for n, v in data.items()}
    out = nc.dram_tensor("out", (T, C), F32, kind="ExternalOutput").ap()
    build(nc, args, out)
    r = _run(nc, [{f"in_{n}": v for n, v in data.items()}], core_ids=[0])
    return r.results[0]["out"].reshape(1, T, C)
```

```python
import math

import concourse.bass as bass
from concourse import mybir
from contextlib import ExitStack

F32 = mybir.dt.float32
F16 = mybir.dt.float16
BF16 = mybir.dt.bfloat16
F8 = mybir.dt.float8e4
ALU = mybir.AluOpType
ACT = mybir.ActivationFunctionType
AX = mybir.AxisListType

P = 128
T = 4096
C = 512
H = 16
D = C // H
R = 8
DS = D - R
I = 1536
CC = C // P
IT = I // P
QT = 512
NT = T // QT
TB = QT // P
NB = T // P
ROWS = 3 * D
THRESHOLD = 0.1
EPS = 1e-5
MASKED = -1e30
LIFT = 18 * math.log(2.0) * math.sqrt(D)
EXP_SCALE = 1.0 / math.sqrt(D)


XN_SCALE = 256.0
W_TOP = 4096.0
FUSE_TOP = 32768.0
FP8_SLACK = 1.0625
NQK = 2 * CC
NACC = NQK + 2 * TB
NPRE = 3 * CC
PAIR_PARTS = ((0, 0), (0, 1), (1, 0))


def token_phase(nc, a, keep, scratch):
    with ExitStack() as ctx:
        sem = lambda name: ctx.enter_context(nc.semaphore(name))
        sb = lambda name, shape, dt: ctx.enter_context(nc.sbuf_tensor(name, shape, dt))
        w_qk = sb("w_qk_sb", [P, 2, 2, CC, C], F16)
        w_v = sb("w_v_sb", [P, 2, CC, C], F16)
        gate_up = sb("gate_up", [P, 2, CC, I], BF16)
        down = sb("down", [P, IT, C], BF16)
        gu_scale = sb("gu_scale_sb", [P, 2, IT], F32)
        down_scale = sb("down_scale_sb", [P, C], F32)
        v_parts = sb("v_parts", [P, 2, H, 4, D], BF16)
        fuse_part = sb("fuse_part", [P, 2, IT, QT], F16)
        xn = sb("xn", [P, TB, C], F32)
        xt_part = sb("xt_part", [P, 2, CC, QT], F16)
        qk_part = sb("qk_part", [P, 2, 2, QT], F16)
        v_rest = sb("v_rest", [P, 2, C], F32)
        ffn_out = v_rest
        gate = sb("gate", [P, 2, QT], F32)
        fuse = sb("fuse", [P, 2, QT], F32)
        stage = sb("stage", [P, 2, I], F32)
        stage8 = fuse[:, :, :].rearrange("p k t -> p (k t)").bitcast(F8)\
            .rearrange("p (k t) -> p k t", k=2)[:, :, 0:I]
        raw = fuse_part[:, :, :, :].rearrange("p k i t -> p (k i t)").bitcast(F32)\
            .rearrange("p (m c f) -> p m c f", m=3, c=CC)
        low_t = [t[:, k, :].rearrange("p (c h r) -> p c h r", c=CC, h=H) for t in (gate, fuse) for k in (0, 1)]
        stats = sb("stats", [P, TB, 6], F32)
        moments = sb("moments", [P, NB, 2], F32)
        var_eps = sb("var_eps", [P, NB], F32)
        root = sb("root", [P, NB], F32)
        rstd = sb("rstd", [P, NB], F32)
        head_w = sb("head_w", [P, H], F32)
        use_ra = sb("use_ra", [P, 2, H], F32)
        feat = sb("feat", [P, 8, CC], F32)
        feat_step = sb("feat_step", [P, 2, CC], F32)
        slab_max = sb("slab_max", [P, 2 * CC], F32)
        up_scale = sb("up_scale", [P, IT], F32)
        peak = sb("peak", [P, 2, 7], F32)
        factor = sb("factor", [P, 8], F32)
        ps = [ctx.enter_context(nc.psum_tensor(f"tok_ps{n}", [P, QT], F32)) for n in range(8)]
        turn = ps[0:2]
        acc = ps[2:4]
        gu = [ps[4:6], ps[6:8]]

        x_in = [sem(f"x_in{t}") for t in range(NT)]
        small_in = sem("small_in")
        raw_in = [sem("raw_q_in"), sem("raw_k_in"), sem("raw_v_in")]
        slab_in = [sem("slab_in0"), sem("slab_in1")]
        slab_cast = sem("slab_cast")
        slab_peak = sem("slab_peak")
        wide_act = sem("wide_act")
        wide_pool = sem("wide_pool")
        const_zero = sem("const_zero")
        const_done = sem("const_done")
        step = sem("step")
        feat_root = sem("feat_root")
        var_ready = sem("var_ready")
        root_ready = sem("root_ready")
        peak_ready = sem("peak_ready")
        peak_all = sem("peak_all")
        swapped = sem("swapped")
        w_factor = sem("w_factor")
        factors_ready = sem("factors_ready")
        w_high = sem("w_high")
        w_split = sem("w_split")
        xn_ready = sem("xn_ready")
        turned = sem("turned")
        xt_high = sem("xt_high")
        xt_low = sem("xt_low")
        acc_ready = sem("acc_ready")
        high_ready = sem("high_ready")
        qk_low = sem("qk_low")
        v_left = sem("v_left")
        v_mid = sem("v_mid")
        v_low = sem("v_low")
        qk_saved = [sem("qk_saved0"), sem("qk_saved1")]
        v_saved = [sem("v_saved0"), sem("v_saved1")]
        gate_ready = sem("gate_ready")
        up_ready = sem("up_ready")
        silu_ready = sem("silu_ready")
        fuse_ready = sem("fuse_ready")
        fuse_high = sem("fuse_high")
        fuse_low = sem("fuse_low")
        down_scaled = sem("down_scaled")

        slabs = [(a["gate_w"], 0, c) for c in range(CC)] + [(a["up_w"], 1, c) for c in range(CC)] \
            + [(a["down_w"], 2, c) for c in range(CC)]

        def slab_source(n):
            w, kind, c = slabs[n]
            if kind < 2:
                return w[c * P:(c + 1) * P, :]
            return w[c * 3 * P:(c + 1) * 3 * P, :].rearrange("(i p) n -> p i n", p=P)

        def slab_target(n):
            _, kind, c = slabs[n]
            if kind < 2:
                return gate_up[:, kind, c, :]
            return down[:, 3 * c:3 * c + 3, :].rearrange("p i n -> p (i n)")

        def by_head(flat):
            return flat.rearrange("p (h d) -> p h d", h=H)

        block = ctx.enter_context(nc.Block())

        @block.sync
        def _(sp):
            def load_x(t):
                sp.dma_start(keep["x"][:, t * TB:(t + 1) * TB, :],
                             a["x"][t * QT:(t + 1) * QT, :].rearrange("(b p) c -> p b c", p=P))\
                    .then_inc(x_in[t], 16)

            load_x(0)
            for m in range(3):
                sp.dma_start(raw[:, m, :, :], a["w_qkv"][m].rearrange("(c p) f -> p c f", p=P))\
                    .then_inc(raw_in[m], 16)
            for t in range(1, NT):
                load_x(t)
            for k in (0, 1):
                sp.sem_inc(qk_saved[k], 32)
                sp.sem_inc(v_saved[k], 16)
            with sp.Fori(0, NT) as t:
                for n in range(NQK):
                    sp.wait_ge(qk_low, t * NQK + (n + 1))
                    for part in (0, 1):
                        sp.dma_start(scratch["qk"][n // CC, part, (n % CC) * P:(n % CC + 1) * P,
                                                   bass.ds(t * QT, QT)],
                                     qk_part[:, n % 2, part, :]).then_inc(qk_saved[n % 2], 16)
                for b in range(TB):
                    sp.wait_ge(v_low, t * TB + (b + 1))
                    sp.dma_start(scratch["v"][bass.ds(t * QT + b * P, P), :, :],
                                 v_parts[:, b % 2, :, :, :].rearrange("p h k d -> p h (k d)"))\
                        .then_inc(v_saved[b % 2], 16)
            for k in (0, 1):
                sp.wait_ge(qk_saved[k], (NT * (NQK // 2) + 1) * 32)
                sp.wait_ge(v_saved[k], (NT * (TB // 2) + 1) * 16)

        @block.gpsimd
        def _(pool):
            for name in ("ident", "ident16", "mask_kq", "mask_qk"):
                nc.gpsimd.memset(keep[name][:, :], 0.0).then_inc(const_zero, 1)
            pool.wait_ge(const_zero, 4)
            for name in ("ident", "ident16"):
                m = keep[name][:, :]
                nc.gpsimd.affine_select(out=m, in_=m, compare_op=ALU.not_equal, fill=1.0, base=0,
                                        pattern=[[-1, P]], channel_multiplier=1).then_inc(const_done, 1)
            for name, sign in (("mask_kq", 1), ("mask_qk", -1)):
                m = keep[name][:, :]
                nc.gpsimd.affine_select(out=m, in_=m, compare_op=ALU.is_ge, fill=MASKED, base=0,
                                        pattern=[[sign, P]], channel_multiplier=-sign)\
                    .then_inc(const_done, 1)
            nc.gpsimd.memset(v_parts[:, :, :, 3, :], 1.0).then_inc(const_done, 1)

            pool.wait_ge(peak_ready, 1)
            nc.gpsimd.partition_all_reduce(peak[:, 1, 0:3], peak[:, 0, 0:3], P,
                                           bass.bass_isa.ReduceOp.max).then_inc(peak_all, 1)
            for n in range(1, NPRE, 2):
                pool.wait_ge(slab_cast, n + 1)
                nc.gpsimd.tensor_copy(slab_target(n), stage8[:, n % 2, :]).then_inc(wide_pool, 1)
                if n == 2 * CC + 1:
                    pool.wait_ge(peak_ready, 2)
                    nc.gpsimd.partition_all_reduce(peak[:, 1, 3:7], peak[:, 0, 3:7], P,
                                                   bass.bass_isa.ReduceOp.max).then_inc(peak_all, 1)

        @block.tensor
        def _(pe):
            def transposes(t, c):
                if c == 0:
                    pe.wait_ge(xn_ready, t * TB + TB)
                if c >= 2:
                    pe.wait_ge(xt_high, t * CC + (c - 1))
                    pe.wait_ge(xt_low, t * CC + (c - 1))
                for b in range(TB):
                    mm = nc.tensor.transpose(turn[c % 2][:, b * P:(b + 1) * P],
                                             xn[:, b, c * P:(c + 1) * P], keep["ident"][:, :])
                mm.then_inc(turned, 1)

            def tile(t, first=False, last=False):
                pe.wait_ge(xt_high, t * CC + CC)
                pe.wait_ge(xt_low, t * CC + CC)
                for n in range(NQK + TB):
                    if n >= NQK + 2:
                        pe.wait_ge(v_left, t * TB + (n - NQK - 1))
                    elif n >= 2:
                        pe.wait_ge(qk_low, t * NQK + (n - 1))
                    elif not first:
                        pe.wait_ge(down_scaled, t * TB + (n - 1))
                    if first and n in (0, CC, NQK):
                        pe.wait_ge(w_split, n // CC + 1)
                    for c in range(CC):
                        for m, (wp, xp) in enumerate(PAIR_PARTS):
                            edge = dict(start=(c == 0 and m == 0), stop=(c == CC - 1 and m == 2))
                            if n < NQK:
                                f = n % CC
                                mm = nc.tensor.matmul(acc[n % 2][:, :],
                                                      w_qk[:, n // CC, wp, c, f * P:(f + 1) * P],
                                                      xt_part[:, xp, c, :], **edge)
                            else:
                                b = n - NQK
                                mm = nc.tensor.matmul(acc[n % 2][:, :],
                                                      xt_part[:, xp, c, b * P:(b + 1) * P],
                                                      w_v[:, wp, c, :], **edge)
                    mm.then_inc(acc_ready, 1)
                if first:
                    pe.wait_ge(wide_act, CC)
                    pe.wait_ge(wide_pool, CC)
                for i in range(IT):
                    for k in (0, 1):
                        if i >= 2:
                            pe.wait_ge(fuse_ready if k else silu_ready, t * IT + (i - 1))
                        for c in range(CC):
                            for part in (0, 1):
                                mm = nc.tensor.matmul(gu[k][i % 2][:, :],
                                                      gate_up[:, k, c, i * P:(i + 1) * P],
                                                      xt_part[:, part, c, :],
                                                      start=(c == 0 and part == 0),
                                                      stop=(c == CC - 1 and part == 1))
                        mm.then_inc(up_ready if k else gate_ready, 1)
                if first:
                    pe.wait_ge(wide_act, NPRE // 2)
                    pe.wait_ge(wide_pool, NPRE // 2)
                for b in range(TB):
                    n = NQK + TB + b
                    if b >= 2:
                        pe.wait_ge(down_scaled, t * TB + (b - 1))
                    else:
                        pe.wait_ge(v_left, t * TB + (b + 3))
                    for i in range(IT):
                        if b == 0:
                            if i == 0:
                                pe.wait_ge(fuse_low, t * IT + (IT - 1))
                            if i == IT - 1:
                                pe.wait_ge(fuse_low, t * IT + IT)
                        for part in (0, 1):
                            mm = nc.tensor.matmul(acc[n % 2][:, :],
                                                  fuse_part[:, part, i, b * P:(b + 1) * P],
                                                  down[:, i, :], start=(i == 0 and part == 0),
                                                  stop=(i == IT - 1 and part == 1))
                    mm.then_inc(acc_ready, 1)
                    if not last:
                        for c in ((0, 1), (2,), (3,), ())[b]:
                            transposes(t + 1, c)

            pe.wait_ge(const_done, 5)
            for c in range(CC):
                transposes(0, c)
            tile(0, first=True)
            with pe.Fori(1, NT - 1) as t:
                tile(t)
            tile(NT - 1, last=True)

        @block.scalar
        def _(act):
            def load_slab(n):
                kind = slabs[n][1]
                act.dma_start(stage[:, n % 2, :] if kind < 2
                              else stage[:, n % 2, :].rearrange("p (i n) -> p i n", i=3),
                              slab_source(n)).then_inc(slab_in[n % 2], 16)

            def cast_slab(n):
                act.wait_ge(slab_in[n % 2], 16 * (n // 2 + 1))
                if n >= 3 and n % 2:
                    act.wait_ge(wide_pool, n // 2)
                if n >= 2 and n % 2 == 0:
                    act.wait_ge(wide_act, n // 2)
                nc.scalar.activation(stage8[:, n % 2, :], stage[:, n % 2, :], ACT.Copy, saturate=False)\
                    .then_inc(slab_cast, 1)
                if n % 2 == 0:
                    act.wait_ge(slab_cast, n + 1)
                    nc.scalar.activation(slab_target(n), stage8[:, 0, :], ACT.Copy).then_inc(wide_act, 1)
                if n + 2 < NPRE:
                    act.wait_ge(slab_cast, n + 1)
                    if slabs[n][1] < 2:
                        act.wait_ge(slab_peak, n + 1)
                    load_slab(n + 2)

            def turn_high(t, c):
                act.wait_ge(turned, t * CC + (c + 1))
                nc.scalar.activation(xt_part[:, 0, c, :], turn[c % 2][:, :], ACT.Copy)\
                    .then_inc(xt_high, 1)

            def tile(t, first=False, last=False):
                for n in range(NQK):
                    act.wait_ge(acc_ready, t * NACC + (n + 1))
                    act.wait_ge(qk_saved[n % 2], t * (NQK // 2 * 32) + (n // 2 + 1) * 32)
                    nc.scalar.activation(qk_part[:, n % 2, 0, :], acc[n % 2][:, :], ACT.Copy,
                                         scale=feat[:, 0, n % CC:n % CC + 1]).then_inc(high_ready, 1)
                    if first:
                        cast_slab(n)
                for b in range(TB):
                    act.wait_ge(acc_ready, t * NACC + (NQK + b + 1))
                    act.wait_ge(v_saved[b % 2], t * (TB // 2 * 16) + (b // 2 + 1) * 16)
                    nc.scalar.activation(v_parts[:, b % 2, :, 0, :], by_head(acc[b % 2][:, :]),
                                         ACT.Copy, scale=factor[:, 1:2]).then_inc(high_ready, 1)
                    act.wait_ge(v_left, t * TB + (b + 1))
                    nc.scalar.activation(v_parts[:, b % 2, :, 1, :], by_head(v_rest[:, b % 2, :]),
                                         ACT.Copy).then_inc(v_mid, 1)
                    if first:
                        cast_slab(NQK + b)
                for i in range(IT + 1):
                    if i < IT:
                        act.wait_ge(gate_ready, t * IT + (i + 1))
                        if i >= 2:
                            act.wait_ge(fuse_ready, t * IT + (i - 1))
                        nc.scalar.activation(gate[:, i % 2, :], gu[0][i % 2][:, :], ACT.Silu,
                                             scale=gu_scale[:, 0, i:i + 1]).then_inc(silu_ready, 1)
                    if i >= 1:
                        act.wait_ge(fuse_ready, t * IT + i)
                        nc.scalar.activation(fuse_part[:, 0, i - 1, :], fuse[:, (i - 1) % 2, :],
                                             ACT.Copy).then_inc(fuse_high, 1)
                    if first and i == TB * 2:
                        act.wait_ge(var_ready, 2)
                        nc.scalar.activation(root[:, TB:NB], var_eps[:, TB:NB], ACT.Sqrt)\
                            .then_inc(root_ready, 1)
                if not last:
                    for c in range(CC):
                        turn_high(t + 1, c)
                act.wait_ge(acc_ready, t * NACC + NACC)

            act.dma_start(head_w[:, :], a["w_rec"].partition_broadcast(P)).then_inc(small_in, 16)
            act.dma_start(feat[:, 2:5, :], a["w_feat"]).then_inc(small_in, 16)
            act.dma_start(gu_scale[:, :, :], a["gu_scale"]).then_inc(small_in, 16)
            act.dma_start(down_scale[:, :], a["down_scale"].partition_broadcast(P)).then_inc(small_in, 16)
            load_slab(0)
            load_slab(1)
            act.wait_ge(var_ready, 1)
            nc.scalar.activation(root[:, 0:TB], var_eps[:, 0:TB], ACT.Sqrt).then_inc(root_ready, 1)
            act.wait_ge(step, 1)
            nc.scalar.activation(feat[:, 5:7, :], feat[:, 2:4, :], ACT.Sqrt).then_inc(feat_root, 1)
            act.wait_ge(w_factor, 1)
            act.wait_ge(swapped, 2)
            for c in range(CC):
                if c == 0:
                    for m in (0, 1, 2):
                        target = w_qk[:, m, 0, :, :] if m < 2 else w_v[:, 0, :, :]
                        act.wait_ge(raw_in[m], 16)
                        nc.scalar.activation(target, raw[:, m, :, :], ACT.Copy, scale=factor[:, 0:1])\
                            .then_inc(w_high, 1)
                turn_high(0, c)
            act.wait_ge(factors_ready, 1)
            tile(0, first=True)
            with act.Fori(1, NT - 1) as t:
                tile(t)
            tile(NT - 1, last=True)

        @block.vector
        def _(dve):
            steps = [0]

            def then_step(ins):
                steps[0] += 1
                ins.then_inc(step, 1)
                dve.wait_ge(step, steps[0])

            def refine_root(r, v, tmp):
                then_step(nc.vector.reciprocal(tmp, r))
                then_step(nc.vector.tensor_tensor(tmp, tmp, v, ALU.mult))
                then_step(nc.vector.tensor_tensor(tmp, tmp, r, ALU.add))
                then_step(nc.vector.tensor_scalar(r, tmp, 0.5, None, ALU.mult))

            def tile_stats(t):
                dve.wait_ge(x_in[t], 16)
                for b in range(TB):
                    ins = nc.vector.bn_stats(stats[:, b, :], keep["x"][:, t * TB + b, :])
                then_step(ins)
                for b in range(TB):
                    ins = nc.vector.bn_aggr(moments[:, t * TB + b, :], stats[:, b, :])
                then_step(ins)

            def variances(lo, hi):
                nc.vector.tensor_scalar(var_eps[:, lo:hi], moments[:, lo:hi, 1], EPS, None, ALU.add)\
                    .then_inc(var_ready, 1)

            def inverse_roots(lo, hi):
                r, tmp = root[:, lo:hi], rstd[:, lo:hi]
                refine_root(r, var_eps[:, lo:hi], tmp)
                then_step(nc.vector.reciprocal(tmp, r))
                then_step(nc.vector.tensor_scalar(tmp, tmp, XN_SCALE, None, ALU.mult))

            def normalise(t, b):
                nc.vector.tensor_scalar(xn[:, b, :], keep["x"][:, bass.ds(t * TB + b, 1), :]
                                        .rearrange("p b c -> p (b c)"),
                                        moments[:, bass.ds(t * TB + b, 1), 0],
                                        rstd[:, bass.ds(t * TB + b, 1)],
                                        ALU.subtract, ALU.mult).then_inc(xn_ready, 1)

            def turn_low(t, c):
                dve.wait_ge(xt_high, t * CC + (c + 1))
                nc.vector.tensor_tensor(xt_part[:, 1, c, :], turn[c % 2][:, :], xt_part[:, 0, c, :],
                                        ALU.subtract).then_inc(xt_low, 1)

            def slab_peaks(n):
                dve.wait_ge(slab_in[n % 2], 16 * (n // 2 + 1))
                nc.vector.tensor_reduce(slab_max[:, n:n + 1], stage[:, n % 2, :], AX.X, ALU.max,
                                        apply_absolute_value=True).then_inc(slab_peak, 1)

            def tile(t, first=False, last=False):
                for n in range(NQK):
                    dve.wait_ge(high_ready, t * (NQK + TB) + (n + 1))
                    nc.vector.scalar_tensor_tensor(out=qk_part[:, n % 2, 1, :], in0=acc[n % 2][:, :],
                                                   scalar=feat[:, 0, n % CC:n % CC + 1],
                                                   in1=qk_part[:, n % 2, 0, :],
                                                   op0=ALU.mult, op1=ALU.subtract)\
                        .then_inc(qk_low, 1)
                    if first and n < 2 * CC:
                        slab_peaks(n)
                for b in range(TB):
                    dve.wait_ge(high_ready, t * (NQK + TB) + (NQK + b + 1))
                    nc.vector.scalar_tensor_tensor(out=by_head(v_rest[:, b % 2, :]),
                                                   in0=by_head(acc[b % 2][:, :]),
                                                   scalar=factor[:, 1:2],
                                                   in1=v_parts[:, b % 2, :, 0, :],
                                                   op0=ALU.mult, op1=ALU.subtract)\
                        .then_inc(v_left, 1)
                    if not last and not first:
                        normalise(t + 1, b)
                    dve.wait_ge(v_mid, t * TB + (b + 1))
                    nc.vector.tensor_tensor(v_parts[:, b % 2, :, 2, :], by_head(v_rest[:, b % 2, :]),
                                            v_parts[:, b % 2, :, 1, :], ALU.subtract)\
                        .then_inc(v_low, 1)
                if first:
                    dve.wait_ge(slab_peak, 2 * CC)
                    nc.vector.reduce_max(peak[:, 0, 3:5], slab_max[:, 0:2 * CC]
                                         .rearrange("p (k c) -> p k c", k=2), AX.X)\
                        .then_inc(peak_ready, 1)
                    dve.wait_ge(peak_all, 2)
                    then_step(nc.vector.tensor_tensor(factor[:, 2:4], peak[:, 1, 3:5], peak[:, 1, 5:7],
                                                      ALU.mult))
                    then_step(nc.vector.tensor_scalar(factor[:, 2:4], factor[:, 2:4],
                                                      C * FP8_SLACK, 1e-15, ALU.mult, ALU.max))
                    then_step(nc.vector.tensor_tensor(factor[:, 4:5], factor[:, 2:3], factor[:, 3:4],
                                                      ALU.mult))
                    then_step(nc.vector.tensor_scalar(factor[:, 4:5], factor[:, 4:5], 1.0 / FUSE_TOP, None,
                                                      ALU.mult))
                    then_step(nc.vector.reciprocal(factor[:, 5:6], factor[:, 4:5]))
                    then_step(nc.vector.tensor_scalar(down_scale[:, :], down_scale[:, :],
                                                      factor[:, 4:5], None, ALU.mult))
                    then_step(nc.vector.tensor_scalar(up_scale[:, :], gu_scale[:, 1, :], factor[:, 5:6],
                                                      1.0 / XN_SCALE, ALU.mult, ALU.mult))
                    dve.wait_ge(wide_act, NPRE // 2)
                    dve.wait_ge(wide_pool, NPRE // 2)
                for i in range(IT + 1):
                    if i < IT:
                        dve.wait_ge(up_ready, t * IT + (i + 1))
                        dve.wait_ge(silu_ready, t * IT + (i + 1))
                        if i >= 2:
                            dve.wait_ge(fuse_low, t * IT + (i - 1))
                        nc.vector.scalar_tensor_tensor(out=fuse[:, i % 2, :], in0=gu[1][i % 2][:, :],
                                                       scalar=up_scale[:, i:i + 1],
                                                       in1=gate[:, i % 2, :], op0=ALU.mult, op1=ALU.mult)\
                            .then_inc(fuse_ready, 1)
                    if i >= 1:
                        dve.wait_ge(fuse_high, t * IT + i)
                        nc.vector.tensor_tensor(fuse_part[:, 1, i - 1, :], fuse[:, (i - 1) % 2, :],
                                                fuse_part[:, 0, i - 1, :], ALU.subtract)\
                            .then_inc(fuse_low, 1)
                    if first:
                        if i < NT - 1:
                            tile_stats(i + 1)
                        if i == NT - 1:
                            variances(TB, NB)
                        if i == IT - 1:
                            dve.wait_ge(root_ready, 2)
                            inverse_roots(TB, NB)
                            for b in range(TB):
                                normalise(1, b)
                for b in range(TB):
                    dve.wait_ge(acc_ready, t * NACC + (NQK + TB + b + 1))
                    nc.vector.tensor_tensor(ffn_out[:, b % 2, :], acc[b % 2][:, :], down_scale[:, :],
                                            ALU.mult).then_inc(down_scaled, 1)
                    dve.wait_ge(down_scaled, t * TB + (b + 1))
                    xb = keep["x"][:, bass.ds(t * TB + b, 1), :].rearrange("p b c -> p (b c)")
                    nc.vector.tensor_tensor(xb, xb, ffn_out[:, b % 2, :], ALU.add)
                    if not last:
                        for c in ((0, 1), (2,), (3,), ())[b]:
                            turn_low(t + 1, c)

            dve.wait_ge(small_in, 64)
            then_step(nc.vector.tensor_scalar(feat[:, 2:4, :], feat[:, 2:4, :], 1e-8, None, ALU.max))
            then_step(nc.vector.tensor_scalar(use_ra[:, 0, :], head_w[:, :], THRESHOLD, None, ALU.is_gt))
            then_step(nc.vector.tensor_scalar(use_ra[:, 1, :], use_ra[:, 0, :], -1.0, 1.0,
                                              ALU.mult, ALU.add))
            then_step(nc.vector.tensor_reduce(peak[:, 0, 5:7], gu_scale[:, :, :], AX.X, ALU.max,
                                              apply_absolute_value=True))
            tile_stats(0)
            variances(0, TB)
            for m in range(3):
                dve.wait_ge(raw_in[m], 16)
                ins = nc.vector.tensor_reduce(peak[:, 0, m:m + 1], raw[:, m, :, :]
                                              .rearrange("p c f -> p (c f)"), AX.X, ALU.max,
                                              apply_absolute_value=True)
            ins.then_inc(peak_ready, 1)
            low = [raw[:, m, :, :].rearrange("p c (h d) -> p c h d", h=H)[:, :, :, DS:D] for m in (0, 1)]
            for k, (m, u) in enumerate(((0, 1), (1, 0), (1, 1), (0, 0))):
                for c in range(CC):
                    ins = nc.vector.tensor_tensor(low_t[k][:, c, :, :], low[m][:, c, :, :],
                                                  use_ra[:, u, :].unsqueeze(2).broadcast_to([P, H, R]),
                                                  ALU.mult)
            then_step(ins)
            for m in (0, 1):
                for c in range(CC):
                    ins = nc.vector.tensor_tensor(low[m][:, c, :, :], low_t[2 * m][:, c, :, :],
                                                  low_t[2 * m + 1][:, c, :, :], ALU.add)
                ins.then_inc(swapped, 1)
            dve.wait_ge(swapped, 2)
            dve.wait_ge(peak_all, 1)
            then_step(nc.vector.reduce_max(factor[:, 6:7], peak[:, 1, 0:3], AX.X))
            then_step(nc.vector.tensor_scalar(factor[:, 6:7], factor[:, 6:7], 1e-30, 1.0 / W_TOP,
                                              ALU.max, ALU.mult))
            nc.vector.tensor_scalar(factor[:, 1:2], factor[:, 6:7], 1.0 / XN_SCALE, None, ALU.mult)
            nc.vector.reciprocal(factor[:, 0:1], factor[:, 6:7]).then_inc(w_factor, 1)
            dve.wait_ge(root_ready, 1)
            inverse_roots(0, TB)
            for b in range(TB):
                normalise(0, b)
            for m in range(3):
                dve.wait_ge(w_high, m + 1)
                high, lowp = ((w_qk[:, m, 0, :, :], w_qk[:, m, 1, :, :]) if m < 2
                              else (w_v[:, 0, :, :], w_v[:, 1, :, :]))
                flat = lambda x: x.rearrange("p c f -> p (c f)")
                nc.vector.scalar_tensor_tensor(out=flat(lowp), in0=flat(raw[:, m, :, :]),
                                               scalar=factor[:, 0:1], in1=flat(high),
                                               op0=ALU.mult, op1=ALU.subtract).then_inc(w_split, 1)
                if m == 0:
                    for c in range(CC):
                        turn_low(0, c)
                    dve.wait_ge(feat_root, 1)
                    refine_root(feat[:, 5:7, :], feat[:, 2:4, :], feat_step[:, :, :])
                    then_step(nc.vector.tensor_scalar(feat[:, 1, :], feat[:, 3, :], THRESHOLD, None,
                                                      ALU.is_gt))
                    then_step(nc.vector.tensor_tensor(feat[:, 7, :], feat[:, 4, :], feat[:, 1, :],
                                                      ALU.mult))
                    then_step(nc.vector.tensor_tensor(feat[:, 6, :], feat[:, 6, :], feat[:, 7, :],
                                                      ALU.mult))
                    then_step(nc.vector.tensor_scalar(feat[:, 7, :], feat[:, 7, :], -1.0, 1.0,
                                                      ALU.mult, ALU.add))
                    then_step(nc.vector.tensor_tensor(feat[:, 5, :], feat[:, 5, :], feat[:, 7, :],
                                                      ALU.mult))
                    then_step(nc.vector.tensor_tensor(feat[:, 5, :], feat[:, 5, :], feat[:, 6, :],
                                                      ALU.add))
                    then_step(nc.vector.tensor_scalar(feat[:, 0, :], feat[:, 5, :], factor[:, 1:2], None,
                                                      ALU.mult))
                    nc.vector.tensor_scalar(gu_scale[:, 0, :], gu_scale[:, 0, :],
                                            1.0 / XN_SCALE, None, ALU.mult).then_inc(factors_ready, 1)
            tile(0, first=True)
            with dve.Fori(1, NT - 1) as t:
                tile(t)
            tile(NT - 1, last=True)


def score_pairs():
    pairs = []
    for i in range(NT):
        for j in range(0, TB * i, 2):
            pairs.append((i, [(j, 0, 0, QT, False), (j + 1, 0, QT, QT, False)]))
        j = TB * i
        pairs.append((i, [(j, 0, 0, QT, True), (j + 1, P, QT, QT - P, True)]))
        pairs.append((i, [(j + 2, 2 * P, 0, QT - 2 * P, True), (j + 3, 3 * P, 2 * P, QT - 3 * P, True)]))
    return pairs


def max_chunks():
    chunks = []
    for r in range(NB):
        for k in range(0, (r + 1) * P, QT):
            width = min(QT, (r + 1) * P - k)
            chunks.append((r, k, width, k + width == (r + 1) * P))
    return chunks


PAIRS = score_pairs()
CHUNKS = max_chunks()
NPAIR = len(PAIRS)
NIT = 2 * NPAIR
NCHUNK = len(CHUNKS)
FIRST_SLOT = 4
LAST_SLOT = NPAIR - 6
PV_LAG = 2
OUT_LAG = 1
NP_BUF = 4
SPLIT = 640


def chunks_at(slot):
    span = LAST_SLOT - FIRST_SLOT
    lo, hi = (min(max((s - FIRST_SLOT) * NCHUNK // span, 0), NCHUNK) for s in (slot, slot + 1))
    return range(lo, hi)


def attention_phase(nc, keep, scratch):
    with ExitStack() as ctx:
        sem = lambda name: ctx.enter_context(nc.semaphore(name))
        sb = lambda name, shape, dt: ctx.enter_context(nc.sbuf_tensor(name, shape, dt))
        q_sb = [sb(f"q_sb{k}", [P, T], F16) for k in (0, 1)]
        k_sb = [sb(f"k_sb{k}", [P, T], F16) for k in (0, 1)]
        v_sb = [sb(f"v_sb{k}", [P, NB, P], BF16) for k in (0, 1)]
        probs = sb("probs", [P, NP_BUF, 2 * QT], F32)
        probs_low = sb("probs_low", [P, NP_BUF, 2 * QT], F16)
        out_sb = sb("out_sb", [P, 2, QT], F32)
        row_max = sb("row_max", [P, NB, NT], F32)
        head_max = sb("head_max", [P, NB], F32)
        shift = sb("shift", [NB, P], F16)
        scores = [ctx.enter_context(nc.psum_tensor(f"scores{n}", [P, 2 * QT], F32)) for n in (0, 1)]
        search = [ctx.enter_context(nc.psum_tensor(f"search{n}", [P, QT], F32)) for n in (0, 1)]
        out_ps = [ctx.enter_context(nc.psum_tensor(f"out_ps{n}", [P, QT], F32)) for n in (0, 1)]
        probs_high = probs[:, :, :].rearrange("p b q -> p (b q)").bitcast(BF16)\
            .rearrange("p (b q two) -> p b q two", b=NP_BUF, two=2)

        filled = sem("filled")
        qk_loaded = [sem("qk_loaded0"), sem("qk_loaded1")]
        v_loaded = [sem("v_loaded0"), sem("v_loaded1")]
        shift_loaded = [sem("shift_loaded0"), sem("shift_loaded1")]
        scores_ready = sem("scores_ready")
        exp_done = sem("exp_done")
        low_pool = sem("low_pool")
        low_dve = sem("low_dve")
        pv_done = sem("pv_done")
        out_copied = sem("out_copied")
        out_saved = [sem("out_saved0"), sem("out_saved1")]
        search_ready = sem("search_ready")
        search_used = sem("search_used")
        max_ready = sem("max_ready")
        max_turned = sem("max_turned")
        shift_ready = sem("shift_ready")

        block = ctx.enter_context(nc.Block())

        def pe_search(pe, base, b, c):
            r, k, width, diag = CHUNKS[c]
            bank = search[c % 2]
            if c == 0:
                pe.wait_ge(qk_loaded[b], base["loads"][b])
                if base is not first:
                    pe.wait_ge(shift_ready, base["head"])
            if c >= 2:
                pe.wait_ge(search_used, base["chunk"] + (c - 1))
            mm = nc.tensor.matmul(bank[:, 0:width], q_sb[b][0:ROWS, r * P:(r + 1) * P],
                                  k_sb[b][0:ROWS, k:k + width], start=True, stop=not diag)
            if diag:
                mm = nc.tensor.matmul(bank[:, width - P:width], keep["ident16"][:, :],
                                      keep["mask_qk"][:, :], start=False, stop=True)
            mm.then_inc(search_ready, 1)

        def dve_search(dve, base, c):
            r, k, width, _ = CHUNKS[c]
            dve.wait_ge(search_ready, base["chunk"] + (c + 1))
            nc.vector.reduce_max(row_max[:, r, k // QT:k // QT + 1], search[c % 2][:, 0:width], AX.X)\
                .then_inc(search_used, 1)

        def dve_max(dve, base):
            dve.wait_ge(search_used, base["chunk"] + NCHUNK)
            nc.vector.reduce_max(head_max[:, :], row_max[:, :, :], AX.X).then_inc(max_ready, 1)

        def pe_turn(pe, base):
            pe.wait_ge(max_ready, base["head"] + 1)
            nc.tensor.transpose(search[0][0:NB, 0:P], head_max[:, :], keep["ident"][:, :])\
                .then_inc(max_turned, 1)

        def dve_shift(dve, base, b):
            dve.wait_ge(max_turned, base["head"] + 1)
            dve.wait_ge(shift_loaded[1 - b], base["shifts"][1 - b])
            nc.vector.tensor_scalar(shift[:, :], search[0][0:NB, 0:P], -1.0, LIFT, ALU.mult, ALU.add)\
                .then_inc(shift_ready, 1)

        def sp_shift(sp, base, b):
            sp.wait_ge(shift_ready, base["head"] + 1)
            sp.dma_start(q_sb[b][ROWS:ROWS + 1, :],
                         shift[:, :]).then_inc(shift_loaded[b], 16)

        def sp_load(sp, head, b):
            rows = bass.ds(head * D, D)
            for at, part in ((0, 0), (1, 0), (2, 1)):
                sp.dma_start(q_sb[b][at * D:(at + 1) * D, :], scratch["qk"][0, part, rows, :])\
                    .then_inc(qk_loaded[b], 16)
            for at, part in ((0, 0), (1, 1), (2, 0)):
                sp.dma_start(k_sb[b][at * D:(at + 1) * D, :], scratch["qk"][1, part, rows, :])\
                    .then_inc(qk_loaded[b], 16)

        def sp_load_v(sp, head, b):
            sp.dma_start(v_sb[b][:, :, :], scratch["v"].rearrange("(n p) h m -> p n h m", p=P)
                         [:, :, bass.ds(head, 1), :].rearrange("p n h m -> p n (h m)"))\
                .then_inc(v_loaded[b], 16)

        def search_base(it, s):
            b = 1 - s
            return {"chunk": it * (2 * NCHUNK) + (s + 1) * NCHUNK, "head": it * 2 + (s + 1),
                    "loads": {b: it * 96 + (1 if s == 0 else 2) * 96},
                    "shifts": {s: it * 16 + 16}}

        first = {"chunk": 0, "head": 0, "loads": {0: 96}, "shifts": {1: 0}}

        @block.gpsimd
        def _(pool):
            for b in (0, 1):
                nc.gpsimd.memset(k_sb[b][ROWS:ROWS + 1, :], 1.0).then_inc(filled, 1)
                pool.wait_ge(filled, b + 1)
            nc.gpsimd.memset(row_max[:, :, :], MASKED).then_inc(filled, 1)
            with pool.Fori(0, H // 2) as it:
                for n in range(NIT):
                    pool.wait_ge(exp_done, it * NIT + (n + 1))
                    pool.wait_ge(pv_done, it * NIT + (n + 1))
                    width = min(SPLIT, width_of(n))
                    nc.gpsimd.tensor_tensor(probs_low[:, n % NP_BUF, 0:width],
                                            probs[:, n % NP_BUF, 0:width],
                                            probs_high[:, n % NP_BUF, 0:width, 1],
                                            ALU.subtract).then_inc(low_pool, 1)

        @block.tensor
        def _(pe):
            pe.sem_inc(pv_done, NP_BUF)
            pe.wait_ge(filled, 3)
            for c in range(NCHUNK):
                pe_search(pe, first, 0, c)
            pe_turn(pe, first)

            def score_pair(it, n):
                head, k = divmod(n, NPAIR)
                s = head % 2
                if k == 0:
                    pe.wait_ge(shift_loaded[s], it * 16 + (head // 2 + 1) * 16)
                if n >= 2:
                    pe.wait_ge(exp_done, it * NIT + (n - 1))
                i, steps = PAIRS[k]
                for j, q0, col, width, diag in steps:
                    out = scores[n % 2][:, col:col + width]
                    mm = nc.tensor.matmul(out, k_sb[s][0:ROWS + 1, j * P:(j + 1) * P],
                                          q_sb[s][0:ROWS + 1, i * QT + q0:(i + 1) * QT],
                                          start=True, stop=not diag)
                    if diag:
                        mm = nc.tensor.matmul(out[:, 0:P], keep["ident16"][:, :],
                                              keep["mask_kq"][:, :], start=False, stop=True)
                mm.then_inc(scores_ready, 1)

            def product_step(it, n, x):
                head, k = divmod(n, NPAIR)
                s = head % 2
                i, steps = PAIRS[k]
                tile = head * NT + i
                j, q0, col, width, _ = steps[x]
                if x == 0:
                    if k == 0:
                        pe.wait_ge(v_loaded[s], it * 16 + (head // 2 + 1) * 16)
                    if j == 0:
                        pe.wait_ge(out_copied, it * (2 * NT) + (tile + 1))
                    pe.wait_ge(low_pool, it * NIT + (n + 1))
                    if width_of(n) > SPLIT:
                        pe.wait_ge(low_dve, it * (2 * NDVE) + (dve_before(n) + 1))
                for part in (0, 1):
                    rhs = (probs_high[:, n % NP_BUF, col:col + width, 1] if part == 0
                           else probs_low[:, n % NP_BUF, col:col + width])
                    mm = nc.tensor.matmul(out_ps[tile % 2][:, q0:QT], v_sb[s][:, j, :], rhs,
                                          start=(j == 0 and part == 0),
                                          stop=(j == TB * (i + 1) - 1 and part == 1))
                if x == len(steps) - 1:
                    mm.then_inc(pv_done, 1)

            def slot(it, n, last=False):
                if n + 1 < NIT or not last:
                    score_pair(it, n + 1)
                head, k = divmod(n, NPAIR)
                base = search_base(it, head) if head < 2 and not (last and head == 1) else None
                work = list(chunks_at(k)) if base else []
                for x in (0, 1):
                    for c in work[x:x + 1]:
                        pe_search(pe, base, 1 - head, c)
                    if n >= PV_LAG:
                        product_step(it, n - PV_LAG, x)
                for c in work[2:]:
                    pe_search(pe, base, 1 - head, c)
                if base and k == LAST_SLOT:
                    pe_turn(pe, base)

            score_pair(0, 0)
            for n in range(PV_LAG):
                slot(0, n)
            with pe.Fori(0, H // 2 - 1) as it:
                for n in range(PV_LAG, NIT + PV_LAG):
                    slot(it, n)
            for n in range(PV_LAG, NIT):
                slot(H // 2 - 1, n, last=True)
            for n in range(NIT - PV_LAG, NIT):
                for x in (0, 1):
                    product_step(H // 2 - 1, n, x)

        @block.vector
        def _(dve):
            dve.wait_ge(filled, 3)
            for c in range(NCHUNK):
                dve_search(dve, first, c)
            dve_max(dve, first)
            dve.wait_ge(max_turned, 1)
            nc.vector.tensor_scalar(shift[:, :], search[0][0:NB, 0:P], -1.0, LIFT, ALU.mult, ALU.add)\
                .then_inc(shift_ready, 1)

            def slot(it, n, last=False):
                head, k = divmod(n, NPAIR)
                base = None if last and head == 1 else search_base(it, head)
                work = list(chunks_at(k)) if base else []
                for c in work[0:1]:
                    dve_search(dve, base, c)
                total = width_of(n)
                if total > SPLIT:
                    dve.wait_ge(exp_done, it * NIT + (n + 1))
                    dve.wait_ge(pv_done, it * NIT + (n + 1))
                    nc.vector.tensor_tensor(probs_low[:, n % NP_BUF, SPLIT:total],
                                            probs[:, n % NP_BUF, SPLIT:total],
                                            probs_high[:, n % NP_BUF, SPLIT:total, 1],
                                            ALU.subtract).then_inc(low_dve, 1)
                for c in work[1:]:
                    dve_search(dve, base, c)
                if base and k == LAST_SLOT - 1:
                    dve_max(dve, base)
                if base and k == LAST_SLOT + 1:
                    dve_shift(dve, base, 1 - head)

            with dve.Fori(0, H // 2 - 1) as it:
                for n in range(NIT):
                    slot(it, n)
            for n in range(NIT):
                slot(H // 2 - 1, n, last=True)

        @block.scalar
        def _(act):
            act.sem_inc(out_copied, 2)

            def exp_pair(it, n):
                act.wait_ge(scores_ready, it * NIT + (n + 1))
                act.wait_ge(pv_done, it * NIT + (n + 1))
                nc.scalar.activation(probs[:, n % NP_BUF, 0:width_of(n)], scores[n % 2][:, 0:width_of(n)],
                                     ACT.Exp, scale=EXP_SCALE).then_inc(exp_done, 1)

            def copy_output(it, n):
                head, k = divmod(n, NPAIR)
                i = PAIRS[k][0]
                if k < NPAIR - 1 and PAIRS[k + 1][0] == i:
                    return
                tile = head * NT + i
                act.wait_ge(pv_done, it * NIT + (n + 1 + NP_BUF))
                act.wait_ge(out_saved[tile % 2], it * (NT * 16) + (tile // 2 + 1) * 16)
                nc.scalar.activation(out_sb[:, tile % 2, :], out_ps[tile % 2][:, :], ACT.Copy)\
                    .then_inc(out_copied, 1)

            LAG = PV_LAG + OUT_LAG
            for n in range(LAG):
                exp_pair(0, n)
            with act.Fori(0, H // 2 - 1) as it:
                for n in range(LAG, NIT + LAG):
                    exp_pair(it, n)
                    copy_output(it, n - LAG)
            for n in range(LAG, NIT + LAG):
                if n < NIT:
                    exp_pair(H // 2 - 1, n)
                copy_output(H // 2 - 1, n - LAG)

        @block.sync
        def _(sp):
            for b in (0, 1):
                sp.sem_inc(out_saved[b], 16)
            for b in (0, 1):
                sp_load(sp, b, b)
                sp_load_v(sp, b, b)
            sp_shift(sp, first, 0)

            def head(it, s, last=False):
                for i in range(NT):
                    tile = s * NT + i
                    if i == NT - 1:
                        if not (last and s == 1):
                            sp_shift(sp, search_base(it, s), 1 - s)
                        if not last:
                            sp.wait_ge(scores_ready, it * NIT + (s + 1) * NPAIR)
                            sp_load(sp, it * 2 + (s + 2), s)
                    sp.wait_ge(out_copied, it * (2 * NT) + (tile + 1 + 2))
                    sp.dma_start(scratch["out"][:, bass.ds(it * (2 * D) + s * D, D), i * QT:(i + 1) * QT],
                                 out_sb[:, tile % 2, :]).then_inc(out_saved[tile % 2], 16)
                if not last:
                    sp.wait_ge(pv_done, it * NIT + ((s + 1) * NPAIR + NP_BUF))
                    sp_load_v(sp, it * 2 + (s + 2), s)

            with sp.Fori(0, H // 2 - 1) as it:
                for s in (0, 1):
                    head(it, s)
            for s in (0, 1):
                head(H // 2 - 1, s, last=True)
            for b in (0, 1):
                sp.wait_ge(out_saved[b], ((H // 2) * NT + 1) * 16)


def width_of(n):
    return sum(st[3] for st in PAIRS[n % NPAIR][1])


def dve_before(n):
    return sum(1 for m in range(n) if width_of(m) > SPLIT)


NDVE = dve_before(NPAIR)


def output_phase(nc, a, keep, scratch, out):
    with ExitStack() as ctx:
        sem = lambda name: ctx.enter_context(nc.semaphore(name))
        sb = lambda name, shape, dt: ctx.enter_context(nc.sbuf_tensor(name, shape, dt))
        w_proj = sb("w_proj", [P, CC, C], F32)
        parts = sb("parts", [P, 2, CC, 4, QT], F32)
        attn = sb("attn", [P, 2, CC, QT], F32)
        ps = [ctx.enter_context(nc.psum_tensor(f"proj_ps{n}", [P, C], F32)) for n in range(4)]
        w_in = sem("w_in")
        parts_in = [sem("parts_in0"), sem("parts_in1")]
        summed = sem("summed")
        attn_step = sem("attn_step")
        proj_ready = sem("proj_ready")
        y_ready = sem("y_ready")
        y_saved = sem("y_saved")
        block = ctx.enter_context(nc.Block())

        def add_tile(dve, t):
            for b in range(t * TB, (t + 1) * TB):
                dve.wait_ge(proj_ready, b + 1)
                nc.vector.tensor_tensor(keep["x"][:, b, :], ps[b % 4][:, :], keep["x"][:, b, :], ALU.add)\
                    .then_inc(y_ready, 1)

        @block.sync
        def _(sp):
            for t in range(NT):
                if t >= 2:
                    sp.wait_ge(attn_step, 3 * (t - 1))
                for c in range(CC):
                    sp.dma_start(parts[:, t % 2, c, :, :],
                                 scratch["out"][:, c * P:(c + 1) * P, t * QT:(t + 1) * QT]
                                 .rearrange("k r q -> r k q")).then_inc(parts_in[t % 2], 16)

        @block.gpsimd
        def _(pool):
            for t in range(NT):
                pool.wait_ge(parts_in[t % 2], 16 * CC * (t // 2 + 1))
                nc.gpsimd.tensor_tensor(parts[:, t % 2, :, 0, :], parts[:, t % 2, :, 0, :],
                                        parts[:, t % 2, :, 1, :], ALU.add).then_inc(summed, 1)

        @block.vector
        def _(dve):
            for t in range(NT):
                dve.wait_ge(parts_in[t % 2], 16 * CC * (t // 2 + 1))
                pt = parts[:, t % 2, :, :, :]
                nc.vector.reciprocal(pt[:, :, 3, :], pt[:, :, 3, :]).then_inc(attn_step, 1)
                dve.wait_ge(summed, t + 1)
                nc.vector.tensor_tensor(pt[:, :, 0, :], pt[:, :, 0, :], pt[:, :, 2, :], ALU.add)\
                    .then_inc(attn_step, 1)
                dve.wait_ge(attn_step, 3 * t + 2)
                if t >= 2:
                    dve.wait_ge(proj_ready, TB * (t - 1))
                nc.vector.tensor_tensor(attn[:, t % 2, :, :], pt[:, :, 0, :], pt[:, :, 3, :], ALU.mult)\
                    .then_inc(attn_step, 1)
                if t >= 1:
                    add_tile(dve, t - 1)
            add_tile(dve, NT - 1)


        @block.tensor
        def _(pe):
            pe.wait_ge(w_in, 16)
            for t in range(NT):
                pe.wait_ge(attn_step, 3 * (t + 1))
                for b in range(t * TB, (t + 1) * TB):
                    if b >= 4:
                        pe.wait_ge(y_ready, b - 3)
                    for c in range(CC):
                        mm = nc.tensor.matmul(ps[b % 4][:, :],
                                              attn[:, t % 2, c, (b % TB) * P:(b % TB + 1) * P],
                                              w_proj[:, c, :], start=(c == 0), stop=(c == CC - 1))
                    mm.then_inc(proj_ready, 1)

        @block.scalar
        def _(act):
            act.dma_start(w_proj[:, :, :], a["w_proj"].rearrange("(c p) f -> p c f", p=P)).then_inc(w_in, 16)
            for t in range(NT):
                act.wait_ge(y_ready, (t + 1) * TB)
                act.dma_start(out[t * QT:(t + 1) * QT, :].rearrange("(b p) c -> p b c", p=P),
                              keep["x"][:, t * TB:(t + 1) * TB, :]).then_inc(y_saved, 16)
            act.wait_ge(y_saved, 16 * NT)


def build(nc, a, out):
    scratch = {
        "qk": nc.dram_tensor("qk_scratch", (2, 2, C, T), F16).ap(),
        "v": nc.dram_tensor("v_scratch", (T, H, P), BF16).ap(),
        "out": nc.dram_tensor("out_scratch", (4, C, T), F32).ap(),
    }
    with ExitStack() as ctx:
        sb = lambda c, name, shape, dt: c.enter_context(nc.sbuf_tensor(name, shape, dt))
        keep = {
            "x": sb(ctx, "x_sb", [P, NB, C], F32),
            "ident": sb(ctx, "ident", [P, P], F32),
            "ident16": sb(ctx, "ident16", [P, P], BF16),
            "mask_kq": sb(ctx, "mask_kq", [P, P], BF16),
            "mask_qk": sb(ctx, "mask_qk", [P, P], BF16),
        }
        token_phase(nc, a, keep, scratch)
        attention_phase(nc, keep, scratch)
        output_phase(nc, a, keep, scratch, out)


def kernel(**inputs):
    import numpy as _np
    import concourse.bacc as _bacc
    from concourse import mybir as _mybir
    from concourse.bass_utils import run_bass_kernel_spmd as _run

    arr = {n: _np.asarray(v) for n, v in inputs.items()}
    w = arr["L0_attn_W_attn"]
    q_std, k_std, v, q_low, k_low = _np.split(w, [H * DS, 2 * H * DS, 2 * H * DS + C, 2 * H * DS + C + H * R])
    by_head = lambda std, low: _np.concatenate(
        [std.reshape(H, DS, C), low.reshape(H, R, C)], axis=1).reshape(C, C).T
    by_feature = lambda w: (_np.repeat(w, D) if w.size == H else w).reshape(CC, P).T
    is_low = (_np.arange(C) % D >= DS).astype(_np.float32)
    data = {
        "x": arr["L0_attn_x"].reshape(T, C),
        "w_qkv": _np.stack([by_head(q_std, q_low), by_head(k_std, k_low), v.T]),
        "w_proj": arr["L0_attn_W_proj"].T,
        "w_rec": arr["L0_attn_w_rec"],
        "w_feat": _np.stack([by_feature(arr["L0_attn_w_std"]), by_feature(arr["L0_attn_w_rec"]),
                             by_feature(is_low)], axis=1),
        "gate_w": arr["L0_ffn_gate_w"],
        "up_w": arr["L0_ffn_up_w"],
        "down_w": arr["L0_ffn_down_w"],
        "gu_scale": _np.stack([arr["L0_ffn_gate_scale"].reshape(IT, P).T,
                               arr["L0_ffn_up_scale"].reshape(IT, P).T], axis=1),
        "down_scale": arr["L0_ffn_down_scale"],
    }
    data = {n: _np.ascontiguousarray(v) for n, v in data.items()}
    nc = _bacc.Bacc("TRN2", target_bir_lowering=False, num_devices=1)
    args = {n: nc.dram_tensor(f"in_{n}", v.shape, _mybir.dt.from_np(v.dtype), kind="ExternalInput").ap()
            for n, v in data.items()}
    out = nc.dram_tensor("out", (T, C), F32, kind="ExternalOutput").ap()
    build(nc, args, out)
    r = _run(nc, [{f"in_{n}": v for n, v in data.items()}], core_ids=[0])
    return r.results[0]["out"].reshape(1, T, C)
```

```python
import math

import concourse.bass as bass
from concourse import mybir
from contextlib import ExitStack

F32 = mybir.dt.float32
F16 = mybir.dt.float16
BF16 = mybir.dt.bfloat16
F8 = mybir.dt.float8e4
ALU = mybir.AluOpType
ACT = mybir.ActivationFunctionType
AX = mybir.AxisListType

P = 128
T = 4096
C = 512
H = 16
D = C // H
R = 8
DS = D - R
I = 1536
CC = C // P
IT = I // P
QT = 512
NT = T // QT
TB = QT // P
NB = T // P
ROWS = 3 * D
THRESHOLD = 0.1
EPS = 1e-5
MASKED = -1e30
LIFT = 18 * math.log(2.0) * math.sqrt(D)
EXP_SCALE = 1.0 / math.sqrt(D)


XN_SCALE = 256.0
W_TOP = 4096.0
FUSE_TOP = 32768.0
FP8_SLACK = 1.0625
NQK = 2 * CC
NACC = NQK + 2 * TB
NPRE = 3 * CC
PAIR_PARTS = ((0, 0), (0, 1), (1, 0))


def token_phase(nc, a, keep, scratch):
    with ExitStack() as ctx:
        sem = lambda name: ctx.enter_context(nc.semaphore(name))
        sb = lambda name, shape, dt: ctx.enter_context(nc.sbuf_tensor(name, shape, dt))
        w_qk = sb("w_qk_sb", [P, 2, 2, CC, C], F16)
        w_v = sb("w_v_sb", [P, 2, CC, C], F16)
        gate_up = sb("gate_up", [P, 2, CC, I], BF16)
        down = sb("down", [P, IT, C], BF16)
        gu_scale = sb("gu_scale_sb", [P, 2, IT], F32)
        down_scale = sb("down_scale_sb", [P, C], F32)
        v_parts = sb("v_parts", [P, 2, H, 4, D], BF16)
        fuse_part = sb("fuse_part", [P, 2, IT, QT], F16)
        xn = sb("xn", [P, TB, C], F32)
        xt_part = sb("xt_part", [P, 2, CC, QT], F16)
        qk_part = sb("qk_part", [P, 2, 2, QT], F16)
        kd_wide = sb("kd_wide", [P, QT // 2], F32)
        kd_part = sb("kd_part", [P, 2, 2, QT // 2], F16)
        v_rest = sb("v_rest", [P, 2, C], F32)
        ffn_out = v_rest
        gate = sb("gate", [P, 2, QT], F32)
        fuse = sb("fuse", [P, 2, QT], F32)
        stage = sb("stage", [P, 2, I], F32)
        stage8 = fuse[:, :, :].rearrange("p k t -> p (k t)").bitcast(F8)\
            .rearrange("p (k t) -> p k t", k=2)[:, :, 0:I]
        raw = fuse_part[:, :, :, :].rearrange("p k i t -> p (k i t)").bitcast(F32)\
            .rearrange("p (m c f) -> p m c f", m=3, c=CC)
        low_t = [t[:, k, :].rearrange("p (c h r) -> p c h r", c=CC, h=H) for t in (gate, fuse) for k in (0, 1)]
        stats = sb("stats", [P, TB, 6], F32)
        moments = sb("moments", [P, NB, 2], F32)
        var_eps = sb("var_eps", [P, NB], F32)
        root = sb("root", [P, NB], F32)
        rstd = sb("rstd", [P, NB], F32)
        head_w = sb("head_w", [P, H], F32)
        use_ra = sb("use_ra", [P, 2, H], F32)
        feat = sb("feat", [P, 8, CC], F32)
        feat_step = sb("feat_step", [P, 2, CC], F32)
        slab_max = sb("slab_max", [P, 2 * CC], F32)
        up_scale = sb("up_scale", [P, IT], F32)
        peak = sb("peak", [P, 2, 7], F32)
        factor = sb("factor", [P, 8], F32)
        ps = [ctx.enter_context(nc.psum_tensor(f"tok_ps{n}", [P, QT], F32)) for n in range(8)]
        turn = ps[0:2]
        acc = ps[2:4]
        gu = [ps[4:6], ps[6:8]]

        x_in = [sem(f"x_in{t}") for t in range(NT)]
        small_in = sem("small_in")
        raw_in = [sem("raw_q_in"), sem("raw_k_in"), sem("raw_v_in")]
        slab_in = [sem("slab_in0"), sem("slab_in1")]
        slab_cast = sem("slab_cast")
        slab_peak = sem("slab_peak")
        wide_act = sem("wide_act")
        wide_pool = sem("wide_pool")
        const_zero = sem("const_zero")
        const_done = sem("const_done")
        step = sem("step")
        feat_root = sem("feat_root")
        var_ready = sem("var_ready")
        root_ready = sem("root_ready")
        peak_ready = sem("peak_ready")
        peak_all = sem("peak_all")
        swapped = sem("swapped")
        w_factor = sem("w_factor")
        factors_ready = sem("factors_ready")
        w_high = sem("w_high")
        w_split = sem("w_split")
        xn_ready = sem("xn_ready")
        turned = sem("turned")
        xt_high = sem("xt_high")
        xt_low = sem("xt_low")
        acc_ready = sem("acc_ready")
        high_ready = sem("high_ready")
        qk_low = sem("qk_low")
        v_left = sem("v_left")
        v_mid = sem("v_mid")
        v_low = sem("v_low")
        qk_saved = [sem("qk_saved0"), sem("qk_saved1")]
        kd_step = sem("kd_step")
        kd_ready = sem("kd_ready")
        kd_saved = sem("kd_saved")
        v_saved = [sem("v_saved0"), sem("v_saved1")]
        gate_ready = sem("gate_ready")
        up_ready = sem("up_ready")
        silu_ready = sem("silu_ready")
        fuse_ready = sem("fuse_ready")
        fuse_high = sem("fuse_high")
        fuse_low = sem("fuse_low")
        down_scaled = sem("down_scaled")

        slabs = [(a["gate_w"], 0, c) for c in range(CC)] + [(a["up_w"], 1, c) for c in range(CC)] \
            + [(a["down_w"], 2, c) for c in range(CC)]

        def slab_source(n):
            w, kind, c = slabs[n]
            if kind < 2:
                return w[c * P:(c + 1) * P, :]
            return w[c * 3 * P:(c + 1) * 3 * P, :].rearrange("(i p) n -> p i n", p=P)

        def slab_target(n):
            _, kind, c = slabs[n]
            if kind < 2:
                return gate_up[:, kind, c, :]
            return down[:, 3 * c:3 * c + 3, :].rearrange("p i n -> p (i n)")

        def by_head(flat):
            return flat.rearrange("p (h d) -> p h d", h=H)

        block = ctx.enter_context(nc.Block())

        @block.sync
        def _(sp):
            def load_x(t):
                sp.dma_start(keep["x"][:, t * TB:(t + 1) * TB, :],
                             a["x"][t * QT:(t + 1) * QT, :].rearrange("(b p) c -> p b c", p=P))\
                    .then_inc(x_in[t], 16)

            load_x(0)
            for m in range(3):
                sp.dma_start(raw[:, m, :, :], a["w_qkv"][m].rearrange("(c p) f -> p c f", p=P))\
                    .then_inc(raw_in[m], 16)
            for t in range(1, NT):
                load_x(t)
            for k in (0, 1):
                sp.sem_inc(qk_saved[k], 32)
                sp.sem_inc(v_saved[k], 16)
            with sp.Fori(0, NT) as t:
                for n in range(NQK):
                    sp.wait_ge(qk_low, t * NQK + (n + 1))
                    for part in (0, 1):
                        sp.dma_start(scratch["qk"][n // CC, part, (n % CC) * P:(n % CC + 1) * P,
                                                   bass.ds(t * QT, QT)],
                                     qk_part[:, n % 2, part, :]).then_inc(qk_saved[n % 2], 16)
                for b in range(TB):
                    sp.wait_ge(v_low, t * TB + (b + 1))
                    sp.dma_start(scratch["v"][bass.ds(t * QT + b * P, P), :, :],
                                 v_parts[:, b % 2, :, :, :].rearrange("p h k d -> p h (k d)"))\
                        .then_inc(v_saved[b % 2], 16)
                    if b % 2 == 1:
                        sp.wait_ge(kd_ready, t * CC + (b + 1))
                        for part in (0, 1):
                            sp.dma_start(scratch["kd"][part, b // 2 * 2 * P:(b // 2 + 1) * 2 * P,
                                                       bass.ds(t * (QT // 2), QT // 2)]
                                         .rearrange("(c p) t -> p c t", p=P),
                                         kd_part[:, part, :, :]).then_inc(kd_saved, 16)
            sp.wait_ge(kd_saved, NT * 64)
            for k in (0, 1):
                sp.wait_ge(qk_saved[k], (NT * (NQK // 2) + 1) * 32)
                sp.wait_ge(v_saved[k], (NT * (TB // 2) + 1) * 16)

        @block.gpsimd
        def _(pool):
            for name in ("ident", "ident16", "mask_kq", "mask_qk"):
                nc.gpsimd.memset(keep[name][:, :], 0.0).then_inc(const_zero, 1)
            pool.wait_ge(const_zero, 4)
            for name in ("ident", "ident16"):
                m = keep[name][:, :]
                nc.gpsimd.affine_select(out=m, in_=m, compare_op=ALU.not_equal, fill=1.0, base=0,
                                        pattern=[[-1, P]], channel_multiplier=1).then_inc(const_done, 1)
            for name, sign in (("mask_kq", 1), ("mask_qk", -1)):
                m = keep[name][:, :]
                nc.gpsimd.affine_select(out=m, in_=m, compare_op=ALU.is_ge, fill=MASKED, base=0,
                                        pattern=[[sign, P]], channel_multiplier=-sign)\
                    .then_inc(const_done, 1)
            nc.gpsimd.memset(v_parts[:, :, :, 3, :], 1.0).then_inc(const_done, 1)

            pool.wait_ge(peak_ready, 1)
            nc.gpsimd.partition_all_reduce(peak[:, 1, 0:3], peak[:, 0, 0:3], P,
                                           bass.bass_isa.ReduceOp.max).then_inc(peak_all, 1)

            def block_differences(t, c, first=False):
                n, m = CC + c, t * CC + c
                even, odd = (qk_part[:, n % 2, :, :].rearrange("p k (j two q) -> p k j two q", two=2, q=P)
                             [:, :, :, x, :] for x in (0, 1))
                by_pair = lambda x: x.rearrange("p (j q) -> p j q", q=P)
                pool.wait_ge(qk_low, t * NQK + (n + 1))
                if not (first and c == 0):
                    pool.wait_ge(kd_ready, m)
                wide, high = by_pair(kd_wide[:, :]), by_pair(kd_part[:, 0, c % 2, :])
                nc.gpsimd.tensor_tensor(wide, even[:, 0, :, :], odd[:, 0, :, :], ALU.subtract)\
                    .then_inc(kd_step, 1)
                pool.wait_ge(kd_step, t * (4 * CC) + (4 * c + 1))
                nc.gpsimd.tensor_tensor(wide, wide, even[:, 1, :, :], ALU.add).then_inc(kd_step, 1)
                pool.wait_ge(kd_step, t * (4 * CC) + (4 * c + 2))
                if c % 2 == 0 and not (first and c == 0):
                    pool.wait_ge(kd_saved, t * 64 + c // 2 * 32)
                nc.gpsimd.tensor_tensor(high, wide, odd[:, 1, :, :], ALU.subtract).then_inc(kd_step, 1)
                pool.wait_ge(kd_step, t * (4 * CC) + (4 * c + 3))
                nc.gpsimd.tensor_tensor(wide, wide, odd[:, 1, :, :], ALU.subtract).then_inc(kd_step, 1)
                pool.wait_ge(kd_step, t * (4 * CC) + (4 * c + 4))
                nc.gpsimd.tensor_tensor(kd_part[:, 1, c % 2, :], kd_wide[:, :], kd_part[:, 0, c % 2, :],
                                        ALU.subtract).then_inc(kd_ready, 1)

            for n in range(1, NPRE, 2):
                pool.wait_ge(slab_cast, n + 1)
                nc.gpsimd.tensor_copy(slab_target(n), stage8[:, n % 2, :]).then_inc(wide_pool, 1)
                for c in {CC - 1: (0,), CC + 1: (1,), NPRE - 1: (2, 3)}.get(n, ()):
                    block_differences(0, c, first=True)
                if n == 2 * CC + 1:
                    pool.wait_ge(peak_ready, 2)
                    nc.gpsimd.partition_all_reduce(peak[:, 1, 3:7], peak[:, 0, 3:7], P,
                                                   bass.bass_isa.ReduceOp.max).then_inc(peak_all, 1)
            with pool.Fori(1, NT) as t:
                for c in range(CC):
                    block_differences(t, c)

        @block.tensor
        def _(pe):
            def transposes(t, c):
                if c == 0:
                    pe.wait_ge(xn_ready, t * TB + TB)
                if c >= 2:
                    pe.wait_ge(xt_high, t * CC + (c - 1))
                    pe.wait_ge(xt_low, t * CC + (c - 1))
                for b in range(TB):
                    mm = nc.tensor.transpose(turn[c % 2][:, b * P:(b + 1) * P],
                                             xn[:, b, c * P:(c + 1) * P], keep["ident"][:, :])
                mm.then_inc(turned, 1)

            def tile(t, first=False, last=False):
                pe.wait_ge(xt_high, t * CC + CC)
                pe.wait_ge(xt_low, t * CC + CC)
                for n in range(NQK + TB):
                    if n >= NQK + 2:
                        pe.wait_ge(v_left, t * TB + (n - NQK - 1))
                    elif n >= 2:
                        pe.wait_ge(qk_low, t * NQK + (n - 1))
                    elif not first:
                        pe.wait_ge(down_scaled, t * TB + (n - 1))
                    if first and n in (0, CC, NQK):
                        pe.wait_ge(w_split, n // CC + 1)
                    for c in range(CC):
                        for m, (wp, xp) in enumerate(PAIR_PARTS):
                            edge = dict(start=(c == 0 and m == 0), stop=(c == CC - 1 and m == 2))
                            if n < NQK:
                                f = n % CC
                                mm = nc.tensor.matmul(acc[n % 2][:, :],
                                                      w_qk[:, n // CC, wp, c, f * P:(f + 1) * P],
                                                      xt_part[:, xp, c, :], **edge)
                            else:
                                b = n - NQK
                                mm = nc.tensor.matmul(acc[n % 2][:, :],
                                                      xt_part[:, xp, c, b * P:(b + 1) * P],
                                                      w_v[:, wp, c, :], **edge)
                    mm.then_inc(acc_ready, 1)
                if first:
                    pe.wait_ge(wide_act, CC)
                    pe.wait_ge(wide_pool, CC)
                for i in range(IT):
                    for k in (0, 1):
                        if i >= 2:
                            pe.wait_ge(fuse_ready if k else silu_ready, t * IT + (i - 1))
                        for c in range(CC):
                            for part in (0, 1):
                                mm = nc.tensor.matmul(gu[k][i % 2][:, :],
                                                      gate_up[:, k, c, i * P:(i + 1) * P],
                                                      xt_part[:, part, c, :],
                                                      start=(c == 0 and part == 0),
                                                      stop=(c == CC - 1 and part == 1))
                        mm.then_inc(up_ready if k else gate_ready, 1)
                if first:
                    pe.wait_ge(wide_act, NPRE // 2)
                    pe.wait_ge(wide_pool, NPRE // 2)
                for b in range(TB):
                    n = NQK + TB + b
                    if b >= 2:
                        pe.wait_ge(down_scaled, t * TB + (b - 1))
                    else:
                        pe.wait_ge(v_left, t * TB + (b + 3))
                    for i in range(IT):
                        if b == 0:
                            if i == 0:
                                pe.wait_ge(fuse_low, t * IT + (IT - 1))
                            if i == IT - 1:
                                pe.wait_ge(fuse_low, t * IT + IT)
                        for part in (0, 1):
                            mm = nc.tensor.matmul(acc[n % 2][:, :],
                                                  fuse_part[:, part, i, b * P:(b + 1) * P],
                                                  down[:, i, :], start=(i == 0 and part == 0),
                                                  stop=(i == IT - 1 and part == 1))
                    mm.then_inc(acc_ready, 1)
                    if not last:
                        for c in ((0, 1), (2,), (3,), ())[b]:
                            transposes(t + 1, c)

            pe.wait_ge(const_done, 5)
            for c in range(CC):
                transposes(0, c)
            tile(0, first=True)
            with pe.Fori(1, NT - 1) as t:
                tile(t)
            tile(NT - 1, last=True)

        @block.scalar
        def _(act):
            def load_slab(n):
                kind = slabs[n][1]
                act.dma_start(stage[:, n % 2, :] if kind < 2
                              else stage[:, n % 2, :].rearrange("p (i n) -> p i n", i=3),
                              slab_source(n)).then_inc(slab_in[n % 2], 16)

            def cast_slab(n):
                act.wait_ge(slab_in[n % 2], 16 * (n // 2 + 1))
                if n >= 3 and n % 2:
                    act.wait_ge(wide_pool, n // 2)
                if n >= 2 and n % 2 == 0:
                    act.wait_ge(wide_act, n // 2)
                nc.scalar.activation(stage8[:, n % 2, :], stage[:, n % 2, :], ACT.Copy, saturate=False)\
                    .then_inc(slab_cast, 1)
                if n % 2 == 0:
                    act.wait_ge(slab_cast, n + 1)
                    nc.scalar.activation(slab_target(n), stage8[:, 0, :], ACT.Copy).then_inc(wide_act, 1)
                if n + 2 < NPRE:
                    act.wait_ge(slab_cast, n + 1)
                    if slabs[n][1] < 2:
                        act.wait_ge(slab_peak, n + 1)
                    load_slab(n + 2)

            def turn_high(t, c):
                act.wait_ge(turned, t * CC + (c + 1))
                nc.scalar.activation(xt_part[:, 0, c, :], turn[c % 2][:, :], ACT.Copy)\
                    .then_inc(xt_high, 1)

            def tile(t, first=False, last=False):
                for n in range(NQK):
                    act.wait_ge(acc_ready, t * NACC + (n + 1))
                    act.wait_ge(qk_saved[n % 2], t * (NQK // 2 * 32) + (n // 2 + 1) * 32)
                    if n >= CC + 2:
                        act.wait_ge(kd_step, t * (4 * CC) + (4 * (n - 2 - CC) + 4))
                    elif n < 2 and not first:
                        act.wait_ge(kd_step, t * (4 * CC) - (4 * (2 - n) - 4))
                    nc.scalar.activation(qk_part[:, n % 2, 0, :], acc[n % 2][:, :], ACT.Copy,
                                         scale=feat[:, 0, n % CC:n % CC + 1]).then_inc(high_ready, 1)
                    if first:
                        cast_slab(n)
                for b in range(TB):
                    act.wait_ge(acc_ready, t * NACC + (NQK + b + 1))
                    act.wait_ge(v_saved[b % 2], t * (TB // 2 * 16) + (b // 2 + 1) * 16)
                    nc.scalar.activation(v_parts[:, b % 2, :, 0, :], by_head(acc[b % 2][:, :]),
                                         ACT.Copy, scale=factor[:, 1:2]).then_inc(high_ready, 1)
                    act.wait_ge(v_left, t * TB + (b + 1))
                    nc.scalar.activation(v_parts[:, b % 2, :, 1, :], by_head(v_rest[:, b % 2, :]),
                                         ACT.Copy).then_inc(v_mid, 1)
                    if first:
                        cast_slab(NQK + b)
                for i in range(IT + 1):
                    if i < IT:
                        act.wait_ge(gate_ready, t * IT + (i + 1))
                        if i >= 2:
                            act.wait_ge(fuse_ready, t * IT + (i - 1))
                        nc.scalar.activation(gate[:, i % 2, :], gu[0][i % 2][:, :], ACT.Silu,
                                             scale=gu_scale[:, 0, i:i + 1]).then_inc(silu_ready, 1)
                    if i >= 1:
                        act.wait_ge(fuse_ready, t * IT + i)
                        nc.scalar.activation(fuse_part[:, 0, i - 1, :], fuse[:, (i - 1) % 2, :],
                                             ACT.Copy).then_inc(fuse_high, 1)
                    if first and i == TB * 2:
                        act.wait_ge(var_ready, 2)
                        nc.scalar.activation(root[:, TB:NB], var_eps[:, TB:NB], ACT.Sqrt)\
                            .then_inc(root_ready, 1)
                if not last:
                    for c in range(CC):
                        turn_high(t + 1, c)
                act.wait_ge(acc_ready, t * NACC + NACC)

            act.dma_start(head_w[:, :], a["w_rec"].partition_broadcast(P)).then_inc(small_in, 16)
            act.dma_start(feat[:, 2:5, :], a["w_feat"]).then_inc(small_in, 16)
            act.dma_start(gu_scale[:, :, :], a["gu_scale"]).then_inc(small_in, 16)
            act.dma_start(down_scale[:, :], a["down_scale"].partition_broadcast(P)).then_inc(small_in, 16)
            load_slab(0)
            load_slab(1)
            act.wait_ge(var_ready, 1)
            nc.scalar.activation(root[:, 0:TB], var_eps[:, 0:TB], ACT.Sqrt).then_inc(root_ready, 1)
            act.wait_ge(step, 1)
            nc.scalar.activation(feat[:, 5:7, :], feat[:, 2:4, :], ACT.Sqrt).then_inc(feat_root, 1)
            act.wait_ge(w_factor, 1)
            act.wait_ge(swapped, 2)
            for c in range(CC):
                if c == 0:
                    for m in (0, 1, 2):
                        target = w_qk[:, m, 0, :, :] if m < 2 else w_v[:, 0, :, :]
                        act.wait_ge(raw_in[m], 16)
                        nc.scalar.activation(target, raw[:, m, :, :], ACT.Copy, scale=factor[:, 0:1])\
                            .then_inc(w_high, 1)
                turn_high(0, c)
            act.wait_ge(factors_ready, 1)
            tile(0, first=True)
            with act.Fori(1, NT - 1) as t:
                tile(t)
            tile(NT - 1, last=True)

        @block.vector
        def _(dve):
            steps = [0]

            def then_step(ins):
                steps[0] += 1
                ins.then_inc(step, 1)
                dve.wait_ge(step, steps[0])

            def refine_root(r, v, tmp):
                then_step(nc.vector.reciprocal(tmp, r))
                then_step(nc.vector.tensor_tensor(tmp, tmp, v, ALU.mult))
                then_step(nc.vector.tensor_tensor(tmp, tmp, r, ALU.add))
                then_step(nc.vector.tensor_scalar(r, tmp, 0.5, None, ALU.mult))

            def tile_stats(t):
                dve.wait_ge(x_in[t], 16)
                for b in range(TB):
                    ins = nc.vector.bn_stats(stats[:, b, :], keep["x"][:, t * TB + b, :])
                then_step(ins)
                for b in range(TB):
                    ins = nc.vector.bn_aggr(moments[:, t * TB + b, :], stats[:, b, :])
                then_step(ins)

            def variances(lo, hi):
                nc.vector.tensor_scalar(var_eps[:, lo:hi], moments[:, lo:hi, 1], EPS, None, ALU.add)\
                    .then_inc(var_ready, 1)

            def inverse_roots(lo, hi):
                r, tmp = root[:, lo:hi], rstd[:, lo:hi]
                refine_root(r, var_eps[:, lo:hi], tmp)
                then_step(nc.vector.reciprocal(tmp, r))
                then_step(nc.vector.tensor_scalar(tmp, tmp, XN_SCALE, None, ALU.mult))

            def normalise(t, b):
                nc.vector.tensor_scalar(xn[:, b, :], keep["x"][:, bass.ds(t * TB + b, 1), :]
                                        .rearrange("p b c -> p (b c)"),
                                        moments[:, bass.ds(t * TB + b, 1), 0],
                                        rstd[:, bass.ds(t * TB + b, 1)],
                                        ALU.subtract, ALU.mult).then_inc(xn_ready, 1)

            def turn_low(t, c):
                dve.wait_ge(xt_high, t * CC + (c + 1))
                nc.vector.tensor_tensor(xt_part[:, 1, c, :], turn[c % 2][:, :], xt_part[:, 0, c, :],
                                        ALU.subtract).then_inc(xt_low, 1)

            def slab_peaks(n):
                dve.wait_ge(slab_in[n % 2], 16 * (n // 2 + 1))
                nc.vector.tensor_reduce(slab_max[:, n:n + 1], stage[:, n % 2, :], AX.X, ALU.max,
                                        apply_absolute_value=True).then_inc(slab_peak, 1)

            def tile(t, first=False, last=False):
                for n in range(NQK):
                    dve.wait_ge(high_ready, t * (NQK + TB) + (n + 1))
                    nc.vector.scalar_tensor_tensor(out=qk_part[:, n % 2, 1, :], in0=acc[n % 2][:, :],
                                                   scalar=feat[:, 0, n % CC:n % CC + 1],
                                                   in1=qk_part[:, n % 2, 0, :],
                                                   op0=ALU.mult, op1=ALU.subtract)\
                        .then_inc(qk_low, 1)
                    if first and n < 2 * CC:
                        slab_peaks(n)
                for b in range(TB):
                    dve.wait_ge(high_ready, t * (NQK + TB) + (NQK + b + 1))
                    nc.vector.scalar_tensor_tensor(out=by_head(v_rest[:, b % 2, :]),
                                                   in0=by_head(acc[b % 2][:, :]),
                                                   scalar=factor[:, 1:2],
                                                   in1=v_parts[:, b % 2, :, 0, :],
                                                   op0=ALU.mult, op1=ALU.subtract)\
                        .then_inc(v_left, 1)
                    if not last and not first:
                        normalise(t + 1, b)
                    dve.wait_ge(v_mid, t * TB + (b + 1))
                    nc.vector.tensor_tensor(v_parts[:, b % 2, :, 2, :], by_head(v_rest[:, b % 2, :]),
                                            v_parts[:, b % 2, :, 1, :], ALU.subtract)\
                        .then_inc(v_low, 1)
                if first:
                    dve.wait_ge(slab_peak, 2 * CC)
                    nc.vector.reduce_max(peak[:, 0, 3:5], slab_max[:, 0:2 * CC]
                                         .rearrange("p (k c) -> p k c", k=2), AX.X)\
                        .then_inc(peak_ready, 1)
                    dve.wait_ge(peak_all, 2)
                    then_step(nc.vector.tensor_tensor(factor[:, 2:4], peak[:, 1, 3:5], peak[:, 1, 5:7],
                                                      ALU.mult))
                    then_step(nc.vector.tensor_scalar(factor[:, 2:4], factor[:, 2:4],
                                                      C * FP8_SLACK, 1e-15, ALU.mult, ALU.max))
                    then_step(nc.vector.tensor_tensor(factor[:, 4:5], factor[:, 2:3], factor[:, 3:4],
                                                      ALU.mult))
                    then_step(nc.vector.tensor_scalar(factor[:, 4:5], factor[:, 4:5], 1.0 / FUSE_TOP, None,
                                                      ALU.mult))
                    then_step(nc.vector.reciprocal(factor[:, 5:6], factor[:, 4:5]))
                    then_step(nc.vector.tensor_scalar(down_scale[:, :], down_scale[:, :],
                                                      factor[:, 4:5], None, ALU.mult))
                    then_step(nc.vector.tensor_scalar(up_scale[:, :], gu_scale[:, 1, :], factor[:, 5:6],
                                                      1.0 / XN_SCALE, ALU.mult, ALU.mult))
                    dve.wait_ge(wide_act, NPRE // 2)
                    dve.wait_ge(wide_pool, NPRE // 2)
                for i in range(IT + 1):
                    if i < IT:
                        dve.wait_ge(up_ready, t * IT + (i + 1))
                        dve.wait_ge(silu_ready, t * IT + (i + 1))
                        if i >= 2:
                            dve.wait_ge(fuse_low, t * IT + (i - 1))
                        nc.vector.scalar_tensor_tensor(out=fuse[:, i % 2, :], in0=gu[1][i % 2][:, :],
                                                       scalar=up_scale[:, i:i + 1],
                                                       in1=gate[:, i % 2, :], op0=ALU.mult, op1=ALU.mult)\
                            .then_inc(fuse_ready, 1)
                    if i >= 1:
                        dve.wait_ge(fuse_high, t * IT + i)
                        nc.vector.tensor_tensor(fuse_part[:, 1, i - 1, :], fuse[:, (i - 1) % 2, :],
                                                fuse_part[:, 0, i - 1, :], ALU.subtract)\
                            .then_inc(fuse_low, 1)
                    if first:
                        if i < NT - 1:
                            tile_stats(i + 1)
                        if i == NT - 1:
                            variances(TB, NB)
                        if i == IT - 1:
                            dve.wait_ge(root_ready, 2)
                            inverse_roots(TB, NB)
                            for b in range(TB):
                                normalise(1, b)
                for b in range(TB):
                    dve.wait_ge(acc_ready, t * NACC + (NQK + TB + b + 1))
                    nc.vector.tensor_tensor(ffn_out[:, b % 2, :], acc[b % 2][:, :], down_scale[:, :],
                                            ALU.mult).then_inc(down_scaled, 1)
                    dve.wait_ge(down_scaled, t * TB + (b + 1))
                    xb = keep["x"][:, bass.ds(t * TB + b, 1), :].rearrange("p b c -> p (b c)")
                    nc.vector.tensor_tensor(xb, xb, ffn_out[:, b % 2, :], ALU.add)
                    if not last:
                        for c in ((0, 1), (2,), (3,), ())[b]:
                            turn_low(t + 1, c)

            dve.wait_ge(small_in, 64)
            then_step(nc.vector.tensor_scalar(feat[:, 2:4, :], feat[:, 2:4, :], 1e-8, None, ALU.max))
            then_step(nc.vector.tensor_scalar(use_ra[:, 0, :], head_w[:, :], THRESHOLD, None, ALU.is_gt))
            then_step(nc.vector.tensor_scalar(use_ra[:, 1, :], use_ra[:, 0, :], -1.0, 1.0,
                                              ALU.mult, ALU.add))
            then_step(nc.vector.tensor_reduce(peak[:, 0, 5:7], gu_scale[:, :, :], AX.X, ALU.max,
                                              apply_absolute_value=True))
            tile_stats(0)
            variances(0, TB)
            for m in range(3):
                dve.wait_ge(raw_in[m], 16)
                ins = nc.vector.tensor_reduce(peak[:, 0, m:m + 1], raw[:, m, :, :]
                                              .rearrange("p c f -> p (c f)"), AX.X, ALU.max,
                                              apply_absolute_value=True)
            ins.then_inc(peak_ready, 1)
            low = [raw[:, m, :, :].rearrange("p c (h d) -> p c h d", h=H)[:, :, :, DS:D] for m in (0, 1)]
            for k, (m, u) in enumerate(((0, 1), (1, 0), (1, 1), (0, 0))):
                for c in range(CC):
                    ins = nc.vector.tensor_tensor(low_t[k][:, c, :, :], low[m][:, c, :, :],
                                                  use_ra[:, u, :].unsqueeze(2).broadcast_to([P, H, R]),
                                                  ALU.mult)
            then_step(ins)
            for m in (0, 1):
                for c in range(CC):
                    ins = nc.vector.tensor_tensor(low[m][:, c, :, :], low_t[2 * m][:, c, :, :],
                                                  low_t[2 * m + 1][:, c, :, :], ALU.add)
                ins.then_inc(swapped, 1)
            dve.wait_ge(swapped, 2)
            dve.wait_ge(peak_all, 1)
            then_step(nc.vector.reduce_max(factor[:, 6:7], peak[:, 1, 0:3], AX.X))
            then_step(nc.vector.tensor_scalar(factor[:, 6:7], factor[:, 6:7], 1e-30, 1.0 / W_TOP,
                                              ALU.max, ALU.mult))
            nc.vector.tensor_scalar(factor[:, 1:2], factor[:, 6:7], 1.0 / XN_SCALE, None, ALU.mult)
            then_step(nc.vector.reciprocal(factor[:, 0:1], factor[:, 6:7]))
            nc.vector.tensor_scalar(keep["v_scale"][:, 0:1], factor[:, 0:1], FUSE_TOP / (C * W_TOP), None,
                                    ALU.mult)
            nc.vector.tensor_scalar(keep["v_scale"][:, 1:2], factor[:, 6:7], C * W_TOP / FUSE_TOP, None,
                                    ALU.mult).then_inc(w_factor, 1)
            dve.wait_ge(root_ready, 1)
            inverse_roots(0, TB)
            for b in range(TB):
                normalise(0, b)
            for m in range(3):
                dve.wait_ge(w_high, m + 1)
                high, lowp = ((w_qk[:, m, 0, :, :], w_qk[:, m, 1, :, :]) if m < 2
                              else (w_v[:, 0, :, :], w_v[:, 1, :, :]))
                flat = lambda x: x.rearrange("p c f -> p (c f)")
                nc.vector.scalar_tensor_tensor(out=flat(lowp), in0=flat(raw[:, m, :, :]),
                                               scalar=factor[:, 0:1], in1=flat(high),
                                               op0=ALU.mult, op1=ALU.subtract).then_inc(w_split, 1)
                if m == 0:
                    for c in range(CC):
                        turn_low(0, c)
                    dve.wait_ge(feat_root, 1)
                    refine_root(feat[:, 5:7, :], feat[:, 2:4, :], feat_step[:, :, :])
                    then_step(nc.vector.tensor_scalar(feat[:, 1, :], feat[:, 3, :], THRESHOLD, None,
                                                      ALU.is_gt))
                    then_step(nc.vector.tensor_tensor(feat[:, 7, :], feat[:, 4, :], feat[:, 1, :],
                                                      ALU.mult))
                    then_step(nc.vector.tensor_tensor(feat[:, 6, :], feat[:, 6, :], feat[:, 7, :],
                                                      ALU.mult))
                    then_step(nc.vector.tensor_scalar(feat[:, 7, :], feat[:, 7, :], -1.0, 1.0,
                                                      ALU.mult, ALU.add))
                    then_step(nc.vector.tensor_tensor(feat[:, 5, :], feat[:, 5, :], feat[:, 7, :],
                                                      ALU.mult))
                    then_step(nc.vector.tensor_tensor(feat[:, 5, :], feat[:, 5, :], feat[:, 6, :],
                                                      ALU.add))
                    then_step(nc.vector.tensor_scalar(feat[:, 0, :], feat[:, 5, :], factor[:, 1:2], None,
                                                      ALU.mult))
                    nc.vector.tensor_scalar(gu_scale[:, 0, :], gu_scale[:, 0, :],
                                            1.0 / XN_SCALE, None, ALU.mult).then_inc(factors_ready, 1)
            tile(0, first=True)
            with dve.Fori(1, NT - 1) as t:
                tile(t)
            tile(NT - 1, last=True)


def score_pairs():
    pairs = []
    for i in range(NT):
        for j in range(0, TB * i, 2):
            pairs.append((i, [(j, 0, 0, QT, False), (j + 1, 0, QT, QT, False)]))
        j = TB * i
        pairs.append((i, [(j, 0, 0, QT, True), (j + 1, P, QT, QT - P, True)]))
        pairs.append((i, [(j + 2, 2 * P, 0, QT - 2 * P, True), (j + 3, 3 * P, 2 * P, QT - 3 * P, True)]))
    return pairs


PAIR_WIDTH = 2 * (QT // P)


def max_chunks():
    chunks = []
    for r in range(NB):
        paired = r // 2 * 2
        for j in range(0, paired, PAIR_WIDTH):
            chunks.append(([r], j, min(PAIR_WIDTH, paired - j), True))
        if r % (2 * TB) == 2 * TB - 2:
            chunks.append((list(range(r - 2 * TB + 2, r + 1, 2)), None, 1, False))
        if r % TB == TB - 1:
            chunks.append(([r - 2, r], None, 2, False))
    return chunks


PAIRS = score_pairs()
CHUNKS = max_chunks()
NPAIR = len(PAIRS)
NIT = 2 * NPAIR
NCHUNK = len(CHUNKS)
PAIRED = [c for c in range(NCHUNK) if CHUNKS[c][3]]
NPAIRED = len(PAIRED)
paired_before = lambda c: sum(1 for p in PAIRED if p < c)
HALVES = [(c, diff) for c in range(NCHUNK) for diff in (True, False) if CHUNKS[c][3] or not diff]
HALF_AT = {half: h for h, half in enumerate(HALVES)}
BANKS = 3
MAXIMA = NB // PAIR_WIDTH + 1
FIRST_SLOT = 4
LAST_SLOT = NPAIR - 6
PV_LAG = 2
OUT_LAG = 1
NP_BUF = 6
PACE = 1.9
LOADS = 9 * 16
RING = 2
HALF = H // 2
LAST_IT = HALF - 1


def width_of(n):
    return sum(st[3] for st in PAIRS[n % NPAIR][1])


def chunk_slots():
    blocks_of = lambda chunk: len(chunk[0]) * chunk[2]
    span = [width_of(n) if FIRST_SLOT <= n < LAST_SLOT else 0 for n in range(NPAIR)]
    total, done, slot, slots = sum(blocks_of(c) for c in CHUNKS), 0, FIRST_SLOT, []
    for chunk in CHUNKS:
        while (done + blocks_of(chunk) / 2) * sum(span) >= total * sum(span[:slot + 1]) and slot < LAST_SLOT - 1:
            slot += 1
        slots.append(slot)
        done += blocks_of(chunk)
    return slots


CHUNK_SLOT = chunk_slots()


def chunks_at(slot):
    return [c for c in range(NCHUNK) if CHUNK_SLOT[c] == slot]


def in_last_head(n, last):
    return last and n >= NPAIR


def split_of(n, last=False):
    width = width_of(n)
    if in_last_head(n, last):
        return min(width, 448)
    searched = sum((CHUNKS[c][2] * P // 2 if CHUNKS[c][3] else QT) + 100 for c in chunks_at(n % NPAIR))
    split = int((searched + width) / (1 + PACE)) // 32 * 32
    return width if width - split < 64 else split


def dve_before(n, last=False):
    return sum(1 for m in range(n) if width_of(m) > split_of(m, last))


NDVE = dve_before(NIT)


EARLY = H - 2
SPREAD = P // H
LATE_SPREAD = 32
EARLY_TILE = 4
FIRST_DUE = 16
PER_TILE = 7
DUE = 12

def tile_end(i):
    return (i + 1) * (i + 2) - 1


def tile_due(i):
    return max(tile_end(i) + DUE, FIRST_DUE + i * PER_TILE) if i >= 0 else 0


def inverse_slot(i):
    return max(tile_end(i) + DUE - 5, tile_due(i - 1) + 4)


def unit_slot(u):
    i, c = divmod(u, CC)
    return tile_due(i - 1) + (c + 1) * (tile_due(i) - tile_due(i - 1)) // CC


NUNIT = NT * CC
units_in = lambda slot: [u for u in range(NUNIT) if unit_slot(u) == slot]
pieces_in = lambda slot: [(i, slot - tile_due(i) - 3) for i in range(NT) if 0 <= slot - tile_due(i) - 3 < TB]
TAIL = tile_due(NT - 1) + 3 + TB + 1


def attention_phase(nc, a, keep, scratch, out):
    with ExitStack() as ctx:
        sem = lambda name: ctx.enter_context(nc.semaphore(name))
        sb = lambda name, shape, dt: ctx.enter_context(nc.sbuf_tensor(name, shape, dt))
        q_sb = [sb(f"q_sb{k}", [P, T], F16) for k in (0, 1)]
        k_sb = [sb(f"k_sb{k}", [P, T], F16) for k in (0, 1)]
        v_sb = [sb(f"v_sb{k}", [P, NB, P], BF16) for k in (0, 1)]
        probs = sb("probs", [P, NP_BUF, 2 * QT], F32)
        probs_low = sb("probs_low", [P, NP_BUF, 2 * QT], F16)
        out_sb = sb("out_sb", [P, 2, QT], F32)
        kd_sb = [sb(f"kd_sb{k}", [P, T // 2], F16) for k in (0, 1)]
        ticket = sb("ticket", [1, 4], F32)
        row_max = sb("row_max", [P, NB, MAXIMA], F32)
        excess = sb("excess", [P, 2, QT], F32)
        head_max = sb("head_max", [P, NB], F32)
        shift = sb("shift", [NB, P], F16)
        w_raw = probs[:, :, :].rearrange("p b q -> p (b q)")[:, 0:CC * C]
        w_proj = sb("w_proj_sb", [P, 2, CC, C], F16)
        late_sums = sb("late_sums", [P, 2, QT // LATE_SPREAD], F32)
        w_peak = sb("w_peak", [P, 2], F32)
        w_factor = sb("w_factor", [P, 3], F32)
        parts = sb("parts", [P, RING, 4, QT], F32)
        early_sums = parts[0:EARLY * SPREAD, 0, 0, :]
        attn = excess
        attn_part = sb("attn_part", [P, 2, 2, CC, QT], F16)
        scores = [ctx.enter_context(nc.psum_tensor(f"scores{n}", [P, QT], F32)) for n in range(BANKS)]
        search = [ctx.enter_context(nc.psum_tensor(f"search{n}", [P, QT], F32)) for n in range(BANKS)]
        out_ps = [ctx.enter_context(nc.psum_tensor(f"out_ps{n}", [P, QT], F32)) for n in (0, 1)]
        probs_high = probs[:, :, :].rearrange("p b q -> p (b q)").bitcast(BF16)\
            .rearrange("p (b q two) -> p b q two", b=NP_BUF, two=2)

        filled = sem("filled")
        qk_loaded = [sem("qk_loaded0"), sem("qk_loaded1")]
        v_loaded = [sem("v_loaded0"), sem("v_loaded1")]
        shift_loaded = [sem("shift_loaded0"), sem("shift_loaded1")]
        scores_ready = sem("scores_ready")
        exp_done = sem("exp_done")
        low_pool = sem("low_pool")
        low_dve = sem("low_dve")
        pv_done = sem("pv_done")
        out_copied = sem("out_copied")
        out_saved = [sem("out_saved0"), sem("out_saved1")]
        diff_ready = sem("diff_ready")
        search_ready = sem("search_ready")
        excess_ready = sem("excess_ready")
        search_used = sem("search_used")
        max_ready = sem("max_ready")
        max_turned = sem("max_turned")
        shift_ready = sem("shift_ready")

        w_in = sem("w_in")
        peak_ready = sem("peak_ready")
        peak_all = sem("peak_all")
        w_step = sem("w_step")
        w_high = sem("w_high")
        w_split = sem("w_split")
        parts_in = [sem(f"parts_in{k}") for k in range(RING)]
        sums_in = sem("sums_in")
        sums_inverted = sem("sums_inverted")
        inverse_saved = sem("inverse_saved")
        parts_added = sem("parts_added")
        out_step = sem("out_step")
        attn_ready = sem("attn_ready")
        attn_high = sem("attn_high")
        attn_low = sem("attn_low")
        proj_ready = sem("proj_ready")
        y_ready = sem("y_ready")
        y_saved = sem("y_saved")

        block = ctx.enter_context(nc.Block())

        def bank_of(base, c, diff):
            banks = search + scores if base is first else search
            return banks[HALF_AT[c, diff] % len(banks)]

        def wait_bank(pe, base, c, diff):
            before = HALF_AT[c, diff] - (2 * BANKS if base is first else BANKS)
            if before >= 0:
                last, was_diff = HALVES[before]
                if was_diff:
                    pe.wait_ge(excess_ready, base["paired"] + (paired_before(last) + 1))
                else:
                    pe.wait_ge(search_used, base["chunk"] + (last + 1))

        def pe_search_diff(pe, base, b, c):
            (r,), j, blocks, _ = CHUNKS[c]
            if c == 0:
                pe.wait_ge(qk_loaded[b], base["loads"][b])
                if base is not first:
                    pe.wait_ge(shift_ready, base["head"])
            wait_bank(pe, base, c, True)
            width = blocks * P // 2
            nc.tensor.matmul(bank_of(base, c, True)[:, 0:width], q_sb[b][0:ROWS, r * P:(r + 1) * P],
                             kd_sb[b][0:ROWS, j * P // 2:j * P // 2 + width], start=True, stop=True)\
                .then_inc(diff_ready, 1)

        def pe_search(pe, base, b, c):
            rows, j, blocks, paired = CHUNKS[c]
            bank = bank_of(base, c, False)
            wait_bank(pe, base, c, False)
            if paired:
                (r,), width = rows, blocks * P // 2
                odd = k_sb[b][0:ROWS, j * P:(j + blocks) * P]\
                    .rearrange("p (j two q) -> p j two q", two=2, q=P)[:, :, 1, :]
                mm = nc.tensor.matmul(bank[:, 0:width].rearrange("p (j q) -> p j q", q=P),
                                      q_sb[b][0:ROWS, r * P:(r + 1) * P], odd, start=True, stop=True)
            else:
                width = blocks * P
                for x, r in enumerate(rows):
                    nc.tensor.matmul(bank[:, x * width:(x + 1) * width], q_sb[b][0:ROWS, r * P:(r + 1) * P],
                                     k_sb[b][0:ROWS, (r + 1) * P - width:(r + 1) * P], start=True, stop=False)
                    mm = nc.tensor.matmul(bank[:, (x + 1) * width - P:(x + 1) * width], keep["ident16"][:, :],
                                          keep["mask_qk"][:, :], start=False, stop=True)
            mm.then_inc(search_ready, 1)

        def act_search(act, base, c):
            width, n = CHUNKS[c][2] * P // 2, paired_before(c)
            act.wait_ge(diff_ready, base["paired"] + (n + 1))
            if n >= 2:
                act.wait_ge(search_used, base["chunk"] + (PAIRED[n - 2] + 1))
            elif base is not first:
                act.wait_ge(search_used, base["chunk"] - (NCHUNK - PAIRED[n - 2] - 1))
            nc.scalar.activation(excess[:, n % 2, 0:width], bank_of(base, c, True)[:, 0:width], ACT.Relu)\
                .then_inc(excess_ready, 1)

        def dve_search(dve, base, c):
            rows, j, blocks, paired = CHUNKS[c]
            bank = bank_of(base, c, False)
            dve.wait_ge(search_ready, base["chunk"] + (c + 1))
            if paired:
                width, n = blocks * P // 2, paired_before(c)
                dve.wait_ge(excess_ready, base["paired"] + (n + 1))
                nc.vector.memset(ticket[:, n % 4:n % 4 + 1], 0.0)
                ins = nc.vector.tensor_tensor_reduce(excess[:, n % 2, 0:width], excess[:, n % 2, 0:width],
                                                     bank[:, 0:width], 1.0, MASKED, ALU.add, ALU.max,
                                                     row_max[:, rows[0], j // PAIR_WIDTH:j // PAIR_WIDTH + 1])
            else:
                ins = nc.vector.reduce_max(row_max[:, rows[0]:rows[-1] + 1:2, MAXIMA - 1],
                                           bank[:, :].rearrange("p (r q) -> p r q", q=blocks * P), AX.X)
            ins.then_inc(search_used, 1)

        def dve_max(dve, base):
            dve.wait_ge(search_used, base["chunk"] + NCHUNK)
            nc.vector.reduce_max(head_max[:, :], row_max[:, :, :], AX.X).then_inc(max_ready, 1)

        def pe_turn(pe, base):
            pe.wait_ge(max_ready, base["head"] + 1)
            nc.tensor.transpose(search[0][0:NB, 0:P], head_max[:, :], keep["ident"][:, :])\
                .then_inc(max_turned, 1)

        def dve_shift(dve, base, b):
            dve.wait_ge(max_turned, base["head"] + 1)
            dve.wait_ge(shift_loaded[1 - b], base["shifts"][1 - b])
            nc.vector.tensor_scalar(shift[:, :], search[0][0:NB, 0:P], -1.0, LIFT, ALU.mult, ALU.add)\
                .then_inc(shift_ready, 1)

        def sp_shift(sp, base, b):
            sp.wait_ge(shift_ready, base["head"] + 1)
            sp.dma_start(q_sb[b][ROWS:ROWS + 1, :],
                         shift[:, :]).then_inc(shift_loaded[b], 16)

        def sp_load(sp, head, b):
            rows = bass.ds(head * D, D)
            for at, part in ((0, 0), (1, 0), (2, 1)):
                sp.dma_start(q_sb[b][at * D:(at + 1) * D, :], scratch["qk"][0, part, rows, :])\
                    .then_inc(qk_loaded[b], 16)
            for at, part in ((0, 0), (1, 1), (2, 0)):
                sp.dma_start(k_sb[b][at * D:(at + 1) * D, :], scratch["qk"][1, part, rows, :])\
                    .then_inc(qk_loaded[b], 16)
                sp.dma_start(kd_sb[b][at * D:(at + 1) * D, :], scratch["kd"][part, rows, :])\
                    .then_inc(qk_loaded[b], 16)

        def sp_load_v(sp, head, b):
            sp.dma_start(v_sb[b][:, :, :], scratch["v"].rearrange("(n p) h m -> p n h m", p=P)
                         [:, :, bass.ds(head, 1), :].rearrange("p n h m -> p n (h m)"))\
                .then_inc(v_loaded[b], 16)

        def search_base(it, s):
            b = 1 - s
            return {"chunk": it * (2 * NCHUNK) + (s + 1) * NCHUNK,
                    "paired": (it * 2 + (s + 1)) * NPAIRED, "head": it * 2 + (s + 1),
                    "loads": {b: it * LOADS + (1 if s == 0 else 2) * LOADS},
                    "shifts": {s: it * 16 + 16}}

        first = {"chunk": 0, "paired": 0, "head": 0, "loads": {0: LOADS}, "shifts": {1: 0}}

        @block.gpsimd
        def _(pool):
            for b in (0, 1):
                nc.gpsimd.memset(k_sb[b][ROWS:ROWS + 1, :], 1.0).then_inc(filled, 1)
                pool.wait_ge(filled, b + 1)
            nc.gpsimd.memset(row_max[:, :, :], MASKED).then_inc(filled, 1)
            pool.wait_ge(peak_ready, 1)
            nc.gpsimd.partition_all_reduce(w_peak[:, 1:2], w_peak[:, 0:1], P,
                                           bass.bass_isa.ReduceOp.max).then_inc(peak_all, 1)

            def low_part(it, n, last=False):
                steps = 1 if split_of(n, last) <= PAIRS[n % NPAIR][1][0][3] else 2
                pool.wait_ge(exp_done, it * (2 * NIT) + (2 * n + steps))
                pool.wait_ge(pv_done, it * NIT + (n + 1))
                width = split_of(n, last)
                nc.gpsimd.tensor_tensor(probs_low[:, n % NP_BUF, 0:width], probs[:, n % NP_BUF, 0:width],
                                        probs_high[:, n % NP_BUF, 0:width, 1], ALU.subtract)\
                    .then_inc(low_pool, 1)

            with pool.Fori(0, LAST_IT) as it:
                for n in range(NIT):
                    low_part(it, n)
            for n in range(NPAIR):
                low_part(LAST_IT, n, last=True)
            for slot in range(TAIL):
                if slot < NPAIR:
                    low_part(LAST_IT, NPAIR + slot, last=True)
                for u in units_in(slot + 1):
                    pool.wait_ge(parts_in[u % RING], 32 * (u // RING + 1))
                    nc.gpsimd.tensor_tensor(parts[:, u % RING, 0, :], parts[:, u % RING, 0, :],
                                            parts[:, u % RING, 1, :], ALU.add).then_inc(parts_added, 1)

        @block.tensor
        def _(pe):
            pe.sem_inc(pv_done, NP_BUF)
            pe.wait_ge(filled, 3)
            for c in range(NCHUNK):
                if CHUNKS[c][3]:
                    pe_search_diff(pe, first, 0, c)
                pe_search(pe, first, 0, c)
            pe_turn(pe, first)

            def score_step(it, n, x):
                head, k = divmod(n, NPAIR)
                s, m = head % 2, 2 * n + x
                if k == 0 and x == 0:
                    pe.wait_ge(shift_loaded[s], it * 16 + (head // 2 + 1) * 16)
                if m >= BANKS:
                    pe.wait_ge(exp_done, it * (2 * NIT) + (m + 1 - BANKS))
                i, steps = PAIRS[k]
                j, q0, _, width, diag = steps[x]
                bank = scores[m % BANKS]
                mm = nc.tensor.matmul(bank[:, 0:width], k_sb[s][0:ROWS + 1, j * P:(j + 1) * P],
                                      q_sb[s][0:ROWS + 1, i * QT + q0:(i + 1) * QT],
                                      start=True, stop=not diag)
                if diag:
                    mm = nc.tensor.matmul(bank[:, 0:P], keep["ident16"][:, :],
                                          keep["mask_kq"][:, :], start=False, stop=True)
                mm.then_inc(scores_ready, 1)

            def product_step(it, n, x, last=False):
                head, k = divmod(n, NPAIR)
                s = head % 2
                i, steps = PAIRS[k]
                tile = head * NT + i
                j, q0, col, width, _ = steps[x]
                if x == 0:
                    if k == 0:
                        pe.wait_ge(v_loaded[s], it * 16 + (head // 2 + 1) * 16)
                    if j == 0:
                        pe.wait_ge(out_copied, it * (2 * NT) + (tile + 1))
                    pe.wait_ge(low_pool, it * NIT + (n + 1))
                    if width_of(n) > split_of(n, last):
                        pe.wait_ge(low_dve, it * NDVE + (dve_before(n, last) + 1))
                for part in (0, 1):
                    rhs = (probs_high[:, n % NP_BUF, col:col + width, 1] if part == 0
                           else probs_low[:, n % NP_BUF, col:col + width])
                    mm = nc.tensor.matmul(out_ps[tile % 2][:, q0:QT], v_sb[s][:, j, :], rhs,
                                          start=(j == 0 and part == 0),
                                          stop=(j == TB * (i + 1) - 1 and part == 1))
                if x == len(steps) - 1:
                    mm.then_inc(pv_done, 1)

            def slot(it, n, last=False):
                head, k = divmod(n, NPAIR)
                base = search_base(it, head) if head < 2 and not (last and head == 1) else None
                work = chunks_at(k) if base else []
                halves = [half for half in HALVES if half[0] in work]
                cuts = [0] + [(len(halves) * x + 2) // 3 for x in (1, 2, 3)]
                for x in (0, 1, 2):
                    if x < 2 and (n + 1 < NIT or not last):
                        score_step(it, n + 1, x)
                    for c, diff in halves[cuts[x]:cuts[x + 1]]:
                        (pe_search_diff if diff else pe_search)(pe, base, 1 - head, c)
                    if x < 2 and n >= PV_LAG:
                        product_step(it, n - PV_LAG, x, last)
                if base and k == LAST_SLOT:
                    pe_turn(pe, base)

            for x in (0, 1):
                score_step(0, 0, x)
            for n in range(PV_LAG):
                slot(0, n)
            with pe.Fori(0, LAST_IT) as it:
                for n in range(PV_LAG, NIT + PV_LAG):
                    slot(it, n)
            for n in range(PV_LAG, NPAIR):
                slot(LAST_IT, n, last=True)
            for n in range(NPAIR, NPAIR + TAIL):
                if n < NIT:
                    slot(LAST_IT, n, last=True)
                elif n < NIT + PV_LAG:
                    for x in (0, 1):
                        product_step(LAST_IT, n - PV_LAG, x, last=True)
                for i, b in pieces_in(n - NPAIR):
                    m = i * TB + b
                    if m == 0:
                        pe.wait_ge(w_split, 1)
                    if b == 0:
                        pe.wait_ge(attn_low, CC * (i + 1))
                    if m >= 2:
                        pe.wait_ge(y_ready, m - 1)
                    for c in range(CC):
                        for p, (ap, wp) in enumerate(PAIR_PARTS):
                            mm = nc.tensor.matmul(search[m % 2][:, :],
                                                  attn_part[:, i % 2, ap, c, b * P:(b + 1) * P],
                                                  w_proj[:, wp, c, :], start=(c == 0 and p == 0),
                                                  stop=(c == CC - 1 and p == 2))
                    mm.then_inc(proj_ready, 1)

        @block.vector
        def _(dve):
            dve.wait_ge(w_in, 16)
            nc.vector.tensor_reduce(w_peak[:, 0:1], w_raw, AX.X, ALU.max, apply_absolute_value=True)\
                .then_inc(peak_ready, 1)
            dve.wait_ge(peak_all, 1)
            nc.vector.tensor_scalar(w_factor[:, 1:2], w_peak[:, 1:2], 1e-30, 1.0 / W_TOP,
                                    ALU.max, ALU.mult).then_inc(w_step, 1)
            dve.wait_ge(w_step, 1)
            nc.vector.reciprocal(w_factor[:, 0:1], w_factor[:, 1:2]).then_inc(w_step, 1)
            nc.vector.tensor_tensor(w_factor[:, 2:3], w_factor[:, 1:2], keep["v_scale"][:, 1:2], ALU.mult)\
                .then_inc(w_step, 1)
            dve.wait_ge(w_high, 1)
            nc.vector.scalar_tensor_tensor(out=w_proj[:, 1, :, :].rearrange("p c f -> p (c f)"),
                                           in0=w_raw, scalar=w_factor[:, 0:1],
                                           in1=w_proj[:, 0, :, :].rearrange("p c f -> p (c f)"),
                                           op0=ALU.mult, op1=ALU.subtract).then_inc(w_split, 1)
            dve.wait_ge(filled, 3)
            for c in range(NCHUNK):
                dve_search(dve, first, c)
            dve_max(dve, first)
            dve.wait_ge(max_turned, 1)
            nc.vector.tensor_scalar(shift[:, :], search[0][0:NB, 0:P], -1.0, LIFT, ALU.mult, ALU.add)\
                .then_inc(shift_ready, 1)

            def slot(it, n, last=False):
                head, k = divmod(n, NPAIR)
                base = None if last and head == 1 else search_base(it, head)
                work = list(chunks_at(k)) if base else []
                total, split = width_of(n), split_of(n, last)
                if total > split:
                    dve.wait_ge(exp_done, it * (2 * NIT) + (2 * n + 2))
                    dve.wait_ge(pv_done, it * NIT + (n + 1))
                    nc.vector.tensor_tensor(probs_low[:, n % NP_BUF, split:total],
                                            probs[:, n % NP_BUF, split:total],
                                            probs_high[:, n % NP_BUF, split:total, 1],
                                            ALU.subtract).then_inc(low_dve, 1)
                for c in work:
                    dve_search(dve, base, c)
                if base and k == LAST_SLOT - 1:
                    dve_max(dve, base)
                if base and k == LAST_SLOT + 1:
                    dve_shift(dve, base, 1 - head)

            def normalise(u):
                part = parts[:, u % RING, :, :]
                dve.wait_ge(parts_added, u + 1)
                nc.vector.tensor_tensor(part[:, 0, :], part[:, 0, :], part[:, 2, :], ALU.add)\
                    .then_inc(out_step, 1)
                dve.wait_ge(out_step, u + 1)
                if u >= 2:
                    dve.wait_ge(attn_low, u - 1)
                nc.vector.scalar_tensor_tensor(out=attn[:, u % 2, :], in0=part[:, 0, :],
                                               scalar=keep["v_scale"][:, 0:1], in1=part[:, 3, :],
                                               op0=ALU.mult, op1=ALU.mult).then_inc(attn_ready, 1)

            def normalised_low(u):
                i, c = divmod(u, CC)
                dve.wait_ge(attn_high, u + 1)
                nc.vector.tensor_tensor(attn_part[:, i % 2, 1, c, :], attn[:, u % 2, :],
                                        attn_part[:, i % 2, 0, c, :], ALU.subtract)\
                    .then_inc(attn_low, 1)

            with dve.Fori(0, LAST_IT) as it:
                for n in range(NIT):
                    slot(it, n)
            for n in range(NPAIR):
                slot(LAST_IT, n, last=True)
                if n == tile_end(EARLY_TILE):
                    dve.wait_ge(sums_in, 16)
                    nc.vector.reciprocal(early_sums, early_sums).then_inc(sums_inverted, 1)
            for k in range(TAIL):
                if k < NPAIR:
                    slot(LAST_IT, NPAIR + k, last=True)
                for i in range(NT):
                    if inverse_slot(i) == k:
                        late = late_sums[0:2 * LATE_SPREAD, i % 2, :]
                        dve.wait_ge(sums_in, 16 * (i + 2))
                        nc.vector.reciprocal(late, late).then_inc(sums_inverted, 1)
                for u in units_in(k - 2):
                    normalised_low(u)
                for u in units_in(k):
                    normalise(u)
                for i, b in pieces_in(k - 1):
                    m = i * TB + b
                    dve.wait_ge(proj_ready, m + 1)
                    nc.vector.scalar_tensor_tensor(out=keep["x"][:, m, :], in0=search[m % 2][:, :],
                                                   scalar=w_factor[:, 2:3], in1=keep["x"][:, m, :],
                                                   op0=ALU.mult, op1=ALU.add).then_inc(y_ready, 1)

        @block.scalar
        def _(act):
            act.sem_inc(out_copied, 2)

            def exp_step(it, n, x):
                _, _, col, width, _ = PAIRS[n % NPAIR][1][x]
                m = 2 * n + x
                act.wait_ge(scores_ready, it * (2 * NIT) + (m + 1))
                if x == 0:
                    act.wait_ge(pv_done, it * NIT + (n + 1))
                nc.scalar.activation(probs[:, n % NP_BUF, col:col + width], scores[m % BANKS][:, 0:width],
                                     ACT.Exp, scale=EXP_SCALE).then_inc(exp_done, 1)

            def copy_output(it, n):
                head, k = divmod(n, NPAIR)
                i = PAIRS[k][0]
                if k < NPAIR - 1 and PAIRS[k + 1][0] == i:
                    return
                tile = head * NT + i
                act.wait_ge(pv_done, it * NIT + (n + 1 + NP_BUF))
                act.wait_ge(out_saved[tile % 2], it * (NT * 16) + (tile // 2 + 1) * 16)
                nc.scalar.activation(out_sb[:, tile % 2, :], out_ps[tile % 2][:, :], ACT.Copy)\
                    .then_inc(out_copied, 1)

            act.dma_start(w_raw.rearrange("p (c f) -> p c f", c=CC),
                          a["w_proj"].rearrange("(c p) f -> p c f", p=P)).then_inc(w_in, 16)
            act.wait_ge(w_step, 2)
            nc.scalar.activation(w_proj[:, 0, :, :].rearrange("p c f -> p (c f)"), w_raw, ACT.Copy,
                                 scale=w_factor[:, 0:1]).then_inc(w_high, 1)
            act.wait_ge(w_split, 1)
            for c in PAIRED:
                act_search(act, first, c)
            LAG = PV_LAG + OUT_LAG
            for n in range(LAG):
                for x in (0, 1):
                    exp_step(0, n, x)

            def slot(it, n):
                head, k = divmod(n - 1, NPAIR)
                work = [c for c in chunks_at(k) if CHUNKS[c][3]] if head < 2 else []
                base = {"chunk": it * (2 * NCHUNK) + (head + 1) * NCHUNK,
                        "paired": (it * 2 + (head + 1)) * NPAIRED} if work else None
                for x, some in enumerate((work[:1], work[1:])):
                    exp_step(it, n, x)
                    if x == 1:
                        copy_output(it, n - LAG)
                    for c in some:
                        act_search(act, base, c)

            with act.Fori(0, LAST_IT) as it:
                for n in range(LAG, NIT + LAG):
                    slot(it, n)
            for n in range(LAG, NPAIR):
                slot(LAST_IT, n)
            for n in range(NPAIR, NPAIR + TAIL):
                if n < NIT:
                    for x in (0, 1):
                        exp_step(LAST_IT, n, x)
                if n < NIT + LAG:
                    copy_output(LAST_IT, n - LAG)
                for i in range(NT):
                    if NPAIR + tile_end(i) == n - LAG:
                        tile = NT + i
                        act.wait_ge(out_copied, LAST_IT * (2 * NT) + (tile + 1 + 2))
                        act.dma_start(scratch["out"][:, (H - 1) * D:H * D, i * QT:(i + 1) * QT],
                                      out_sb[:, tile % 2, :]).then_inc(out_saved[tile % 2], 16)
                for u in units_in(n - NPAIR - 2):
                    i, c = divmod(u, CC)
                    act.wait_ge(attn_ready, u + 1)
                    if i >= 2 and c == 0:
                        act.wait_ge(proj_ready, TB * (i - 1))
                    nc.scalar.activation(attn_part[:, i % 2, 0, c, :], attn[:, u % 2, :], ACT.Copy)\
                        .then_inc(attn_high, 1)

        @block.sync
        def _(sp):
            for b in (0, 1):
                sp.sem_inc(out_saved[b], 16)
            for b in (0, 1):
                sp_load(sp, b, b)
                sp_load_v(sp, b, b)
            sp_shift(sp, first, 0)

            def store_output(it, s, i):
                tile = s * NT + i
                sp.wait_ge(out_copied, it * (2 * NT) + (tile + 1 + 2))
                sp.dma_start(scratch["out"][:, bass.ds(it * (2 * D) + s * D, D), i * QT:(i + 1) * QT],
                             out_sb[:, tile % 2, :]).then_inc(out_saved[tile % 2], 16)

            def head(it, s, load):
                for i in range(NT):
                    if not load and i == EARLY_TILE - 2:
                        for b in (0, 1):
                            sp.wait_ge(out_saved[b], (LAST_IT * NT + 1) * 16)
                        sp.dma_start(early_sums, scratch["out"][3, 0:EARLY * D, :]
                                     .rearrange("(h d) (s q) -> h d s q", d=D, s=SPREAD)[:, 0, :, :])\
                            .then_inc(sums_in, 16)
                    if not load and i == EARLY_TILE + 1:
                        sp.wait_ge(sums_inverted, 1)
                        sp.dma_start(scratch["inverse"][0:EARLY, :].rearrange("h (s q) -> h s q", s=SPREAD),
                                     early_sums).then_inc(inverse_saved, 16)
                    if i == NT - 1:
                        sp_shift(sp, search_base(it, s), 1 - s)
                        if load:
                            sp.wait_ge(scores_ready, it * (2 * NIT) + (s + 1) * (2 * NPAIR))
                            sp_load(sp, it * 2 + (s + 2), s)
                    store_output(it, s, i)
                if load:
                    sp.wait_ge(pv_done, it * NIT + ((s + 1) * NPAIR + NP_BUF))
                    sp_load_v(sp, it * 2 + (s + 2), s)

            def store_y(i):
                sp.wait_ge(y_ready, (i + 1) * TB)
                sp.dma_start(out[i * QT:(i + 1) * QT, :].rearrange("(b p) c -> p b c", p=P),
                             keep["x"][:, i * TB:(i + 1) * TB, :]).then_inc(y_saved, 16)

            with sp.Fori(0, LAST_IT) as it:
                for s in (0, 1):
                    head(it, s, load=True)
            head(LAST_IT, 0, load=False)
            for i in range(NT):
                for c in range(CC):
                    u = i * CC + c
                    if c == CC - 1:
                        sp.wait_ge(out_saved[i % 2], ((HALF * 2 - 1) * (NT // 2) + i // 2 + 2) * 16)
                        if i == 0:
                            sp.wait_ge(out_saved[1], ((HALF * 2 - 1) * (NT // 2) + 1) * 16)
                        late = late_sums[0:2 * LATE_SPREAD, i % 2, :]
                        spread = lambda rows: rows.rearrange("h (s q) -> h s q", s=LATE_SPREAD)
                        sp.dma_start(late, spread(scratch["out"][3, EARLY * D:C, i * QT:(i + 1) * QT]
                                                  .rearrange("(h d) q -> h d q", d=D)[:, 0, :]))\
                            .then_inc(sums_in, 16)
                        sp.wait_ge(sums_inverted, i + 2)
                        sp.dma_start(spread(scratch["inverse"][EARLY:H, i * QT:(i + 1) * QT]), late)\
                            .then_inc(inverse_saved, 16)
                        sp.wait_ge(inverse_saved, 16 * (i + 2))
                    if i == 0 and c == 0:
                        for b in (0, 1):
                            sp.wait_ge(out_saved[b], ((HALF * 2 - 1) * (NT // 2) + 1) * 16)
                        sp.wait_ge(inverse_saved, 16)
                    if u >= RING:
                        sp.wait_ge(attn_ready, u - RING + 1)
                    sp.dma_start(parts[:, u % RING, 0:3, :],
                                 scratch["out"][0:3, c * P:(c + 1) * P, i * QT:(i + 1) * QT]
                                 .rearrange("k r q -> r k q")).then_inc(parts_in[u % RING], 16)
                    heads = P // D
                    sp.dma_start(parts[:, u % RING, 3, :],
                                 scratch["inverse"][c * heads:(c + 1) * heads, i * QT:(i + 1) * QT]
                                 .unsqueeze(1).broadcast_to([heads, D, QT])).then_inc(parts_in[u % RING], 16)
                if i >= 2:
                    store_y(i - 2)
            store_y(NT - 2)
            for m in range(NB - TB, NB):
                sp.wait_ge(y_ready, m + 1)
                sp.dma_start(out[m * P:(m + 1) * P, :], keep["x"][:, m, :]).then_inc(y_saved, 16)
            sp.wait_ge(y_saved, 16 * (NT - 1 + TB))


def build(nc, a, out):
    scratch = {
        "qk": nc.dram_tensor("qk_scratch", (2, 2, C, T), F16).ap(),
        "kd": nc.dram_tensor("kd_scratch", (2, C, T // 2), F16).ap(),
        "v": nc.dram_tensor("v_scratch", (T, H, P), BF16).ap(),
        "out": nc.dram_tensor("out_scratch", (4, C, T), F32).ap(),
        "inverse": nc.dram_tensor("inverse_scratch", (H, T), F32).ap(),
    }
    with ExitStack() as ctx:
        sb = lambda c, name, shape, dt: c.enter_context(nc.sbuf_tensor(name, shape, dt))
        keep = {
            "x": sb(ctx, "x_sb", [P, NB, C], F32),
            "ident": sb(ctx, "ident", [P, P], F32),
            "ident16": sb(ctx, "ident16", [P, P], BF16),
            "mask_kq": sb(ctx, "mask_kq", [P, P], BF16),
            "mask_qk": sb(ctx, "mask_qk", [P, P], BF16),
            "v_scale": sb(ctx, "v_scale", [P, 2], F32),
        }
        token_phase(nc, a, keep, scratch)
        attention_phase(nc, a, keep, scratch, out)


def kernel(**inputs):
    import numpy as _np
    import concourse.bacc as _bacc
    from concourse import mybir as _mybir
    from concourse.bass_utils import run_bass_kernel_spmd as _run

    arr = {n: _np.asarray(v) for n, v in inputs.items()}
    w = arr["L0_attn_W_attn"]
    q_std, k_std, v, q_low, k_low = _np.split(w, [H * DS, 2 * H * DS, 2 * H * DS + C, 2 * H * DS + C + H * R])
    by_head = lambda std, low: _np.concatenate(
        [std.reshape(H, DS, C), low.reshape(H, R, C)], axis=1).reshape(C, C).T
    by_feature = lambda w: (_np.repeat(w, D) if w.size == H else w).reshape(CC, P).T
    is_low = (_np.arange(C) % D >= DS).astype(_np.float32)
    data = {
        "x": arr["L0_attn_x"].reshape(T, C),
        "w_qkv": _np.stack([by_head(q_std, q_low), by_head(k_std, k_low), v.T]),
        "w_proj": arr["L0_attn_W_proj"].T,
        "w_rec": arr["L0_attn_w_rec"],
        "w_feat": _np.stack([by_feature(arr["L0_attn_w_std"]), by_feature(arr["L0_attn_w_rec"]),
                             by_feature(is_low)], axis=1),
        "gate_w": arr["L0_ffn_gate_w"],
        "up_w": arr["L0_ffn_up_w"],
        "down_w": arr["L0_ffn_down_w"],
        "gu_scale": _np.stack([arr["L0_ffn_gate_scale"].reshape(IT, P).T,
                               arr["L0_ffn_up_scale"].reshape(IT, P).T], axis=1),
        "down_scale": arr["L0_ffn_down_scale"],
    }
    data = {n: _np.ascontiguousarray(v) for n, v in data.items()}
    nc = _bacc.Bacc("TRN2", target_bir_lowering=False, num_devices=1)
    args = {n: nc.dram_tensor(f"in_{n}", v.shape, _mybir.dt.from_np(v.dtype), kind="ExternalInput").ap()
            for n, v in data.items()}
    out = nc.dram_tensor("out", (T, C), F32, kind="ExternalOutput").ap()
    build(nc, args, out)
    r = _run(nc, [{f"in_{n}": v for n, v in data.items()}], core_ids=[0])
    return r.results[0]["out"].reshape(1, T, C)
```
